# Optimizing a Trainium2 kernel written in Bass

```python
import numpy as np
import jax
import jax.numpy as jnp

def _softmax(x, axis=-1):
    return jax.nn.softmax(x, axis=axis)

def _gelu(x):
    return jax.nn.gelu(x, approximate=True)

def _silu(x):
    return jax.nn.silu(x)

def _sigmoid(x):
    return jax.nn.sigmoid(x)

def _layernorm(x, axis=-1, eps=1e-05):
    m = jnp.mean(x, axis=axis, keepdims=True)
    v = jnp.var(x, axis=axis, keepdims=True)
    return (x - m) / jnp.sqrt(v + eps)

def _scatter_add(tgt, idx, src, axis=0):
    return tgt.at[idx].add(src)

def _segment_sum(src, seg, n):
    return jax.ops.segment_sum(src, seg, n)
kernel_name = 'mk_xattn_ffn_d1_seqx_r8_b68cb5'

def setup_inputs(seed: int=0):
    np.random.seed(seed)
    _w = jnp.asarray

    def _rec_inputs():
        import jax
        import jax.numpy as jnp
        _rk = jax.random.key(seed)
        x = 7.22e-05 + 1 * jax.random.normal(jax.random.fold_in(_rk, 1), (8, 256, 128), jnp.float32)
        _lenS = 256 - jax.random.randint(jax.random.fold_in(_rk, 7), (8,), 0, max(1, 256 // 4) + 1, jnp.int32)
        _lenS2 = 256 - jax.random.randint(jax.random.fold_in(_rk, 8), (8,), 0, max(1, 256 // 4) + 1, jnp.int32)
        _ctx_1024P = jax.random.normal(jax.random.fold_in(_rk, 11), (8, 16, 128), jnp.float32)
        _ctx_1024c = jax.random.dirichlet(jax.random.fold_in(_rk, 511), 0.3 * jnp.ones((16,), jnp.float32), (8, 256))
        _ctx_1024t = jnp.einsum('bsk,bkd->bsd', _ctx_1024c, _ctx_1024P)
        _ctx_1024t = _ctx_1024t * jax.lax.rsqrt(jnp.mean(jnp.square(_ctx_1024t)) + 1e-12) * 0.953939
        ctx_1024 = 4.13588e-05 + 0.999923 * (_ctx_1024t + 0.3 * jax.random.normal(jax.random.fold_in(_rk, 611), (8, 256, 128), jnp.float32))
        return (x, ctx_1024)
    x, ctx_1024 = _rec_inputs()

    def _L0_xattn_setup():
        import jax, jax.numpy as jnp
        import numpy as np
        DIM = 128
        HEAD_NUM = 8
        D_HEAD = DIM // HEAD_NUM
        B, S = (4, 256)
        key = jax.random.key(seed)
        ks = jax.random.split(key, 7)
        scale = 0.02
        return {'Q': jax.random.normal(ks[0], (B, S, DIM), dtype=jnp.float32), 'K': jax.random.normal(ks[1], (B, S, DIM), dtype=jnp.float32), 'V': jax.random.normal(ks[2], (B, S, DIM), dtype=jnp.float32), 'W_Q': jax.random.normal(ks[3], (DIM, DIM), dtype=jnp.float32) * scale, 'W_K': jax.random.normal(ks[4], (DIM, DIM), dtype=jnp.float32) * scale, 'W_V': jax.random.normal(ks[5], (DIM, DIM), dtype=jnp.float32) * scale, 'W_O': jax.random.normal(ks[6], (DIM, DIM), dtype=jnp.float32) * scale}
    _L0_xattn_all = _L0_xattn_setup()
    _L0_xattn_in = {k: v for k, v in _L0_xattn_all.items() if k in ('W_Q', 'W_K', 'W_V', 'W_O')}
    del _L0_xattn_all

    def _L0_ffn_setup():
        import jax, jax.numpy as jnp
        import numpy as np
        B, T, D, E, K = (2, 256, 128, 8, 2)
        H = 2 * D
        key = jax.random.key(seed)
        ks = jax.random.split(key, 5)
        s = 0.02
        return {'x': jax.random.normal(ks[0], (B, T, D), jnp.float32), 'Wr': jax.random.normal(ks[1], (D, E), jnp.float32) * s, 'br': jnp.zeros((E,), jnp.float32), 'W1': jax.random.normal(ks[2], (E, D, H), jnp.float32) * s, 'b1': jnp.zeros((E, H), jnp.float32), 'W2': jax.random.normal(ks[3], (E, H, D), jnp.float32) * s, 'b2': jnp.zeros((E, D), jnp.float32)}
    _L0_ffn_all = _L0_ffn_setup()
    _L0_ffn_in = {k: v for k, v in _L0_ffn_all.items() if k in ('Wr', 'br', 'W1', 'b1', 'W2', 'b2')}
    del _L0_ffn_all
    return {'x': x, 'ctx_1024': ctx_1024, 'L0_xattn_W_Q': _L0_xattn_in['W_Q'], 'L0_xattn_W_K': _L0_xattn_in['W_K'], 'L0_xattn_W_V': _L0_xattn_in['W_V'], 'L0_xattn_W_O': _L0_xattn_in['W_O'], 'L0_ffn_Wr': _L0_ffn_in['Wr'], 'L0_ffn_br': _L0_ffn_in['br'], 'L0_ffn_W1': _L0_ffn_in['W1'], 'L0_ffn_b1': _L0_ffn_in['b1'], 'L0_ffn_W2': _L0_ffn_in['W2'], 'L0_ffn_b2': _L0_ffn_in['b2']}

def reference(x, ctx_1024, L0_xattn_W_Q, L0_xattn_W_K, L0_xattn_W_V, L0_xattn_W_O, L0_ffn_Wr, L0_ffn_br, L0_ffn_W1, L0_ffn_b1, L0_ffn_W2, L0_ffn_b2):
    import jax
    import jax.numpy as jnp

    def _L0_xattn_ref(Q, K, V, W_Q, W_K, W_V, W_O):
        import jax, jax.numpy as jnp
        import numpy as np
        DIM = 128
        HEAD_NUM = 8
        D_HEAD = DIM // HEAD_NUM
        B, S = (4, 256)
        b, s, d = Q.shape
        h, dh = (HEAD_NUM, d // HEAD_NUM)

        def proj_split(x, W):
            y = jnp.einsum('bsd,ed->bse', x, W)
            return y.reshape(b, s, h, dh).transpose(0, 2, 1, 3)
        q = proj_split(Q, W_Q)
        k = proj_split(K, W_K)
        v = proj_split(V, W_V)
        scores = jnp.einsum('bhqd,bhkd->bhqk', q, k) / jnp.sqrt(jnp.float32(dh))
        attn = jax.nn.softmax(scores, axis=1)
        ctx = jnp.einsum('bhqk,bhkd->bhqd', attn, v)
        ctx = ctx.transpose(0, 2, 1, 3).reshape(b, s, d)
        return jnp.einsum('bsd,ed->bse', ctx, W_O)

    def _L0_ffn_ref(x, Wr, br, W1, b1, W2, b2):
        import jax, jax.numpy as jnp
        import numpy as np
        B, T, D, E, K = (2, 256, 128, 8, 2)
        H = 2 * D
        logits = jnp.einsum('btd,de->bte', x, Wr) + br
        topv, topi = jax.lax.top_k(logits, K)
        sel_mask = jax.nn.one_hot(topi, E, dtype=logits.dtype).sum(-2) > 0
        neg_inf = jnp.finfo(logits.dtype).min
        gates = jax.nn.softmax(jnp.where(sel_mask, logits, neg_inf), axis=-1)
        h = jax.nn.relu(jnp.einsum('btd,edh->bteh', x, W1) + b1)
        out = jnp.einsum('bte,bteh,ehd->btd', gates, h, W2)
        out = out + jnp.einsum('bte,ed->btd', gates, b2)
        return out
    x = x + _L0_xattn_ref(_layernorm(x, axis=-1), ctx_1024, ctx_1024, L0_xattn_W_Q, L0_xattn_W_K, L0_xattn_W_V, L0_xattn_W_O)
    x = x + _L0_ffn_ref(_layernorm(x, axis=-1), L0_ffn_Wr, L0_ffn_br, L0_ffn_W1, L0_ffn_b1, L0_ffn_W2, L0_ffn_b2)
    return x

_drawn_inputs = setup_inputs


def setup_inputs(seed=0):
    import zlib

    import numpy as np

    out = dict(_drawn_inputs(seed))
    spreads = {'L0_ffn_br': (0.0, 0.1), 'L0_ffn_b1': (0.0, 0.686), 'L0_ffn_b2': (0.0, 0.1)}
    factors = {'L0_xattn_W_Q': 2.748, 'L0_xattn_W_K': 2.748}
    for name, (base, spread) in spreads.items():
        noise = np.random.default_rng([zlib.crc32(name.encode()), seed]).standard_normal(out[name].shape)
        drawn = base * np.exp(spread * noise) if base else spread * noise
        out[name] = jnp.asarray(drawn.astype(out[name].dtype))
    for name, factor in factors.items():
        out[name] = (out[name] * factor).astype(out[name].dtype)
    return out
```

```python
from contextlib import ExitStack

import concourse.bass as bass
from concourse import mybir

F32 = mybir.dt.float32
F32R = mybir.dt.float32r
U32 = mybir.dt.uint32
ALU = mybir.AluOpType
ACT = mybir.ActivationFunctionType
AX = mybir.AxisListType

P = 128
EPS = 1e-5


def build(nc, x, ctx_t, w_attn, wr, br, w1, b1_t, w2, b2, out):
    B, S, D = x.shape
    H, DH = 8, D // 8
    E, HID = w1.shape[0], w1.shape[2]
    TT = S // P
    HC = HID // P
    PAIRS = H // 2
    UNITS = TT * TT
    HQ = H * P
    BANK = 512
    SCALE = float(DH) ** -0.5
    STACK_READS = 8
    assert D == P and S == 256 and UNITS == 4

    with ExitStack() as stack:
        def sb(name, shape, dt=F32):
            return stack.enter_context(nc.sbuf_tensor(name, shape, dt))

        def ps(name, shape, dt=F32):
            return stack.enter_context(nc.psum_tensor(name, shape, dt))

        def sem(name):
            return stack.enter_context(nc.semaphore(name))

        ident = sb("ident", [P, P])
        neg_ident = sb("neg_ident", [P, P], F32R)
        iota8 = sb("iota8", [P, E])
        neg_half = sb("neg_half", [P, TT])
        w_qkvo = sb("w_qkvo", [P, 4, D])
        w1_sb = sb("w1_sb", [P, E, HID])
        w1_hi = sb("w1_hi", [P, E, HID], F32R)
        w1_lo = sb("w1_lo", [P, E, HID], F32R)
        b1_sb = sb("b1_sb", [P, E * HC])
        w2_sb = sb("w2_sb", [P, E * HC, D])
        b2_sb = sb("b2_sb", [E, D])
        wr_sb = sb("wr_sb", [P, E])
        wr_hi = sb("wr_hi", [P, E], F32R)
        wr_lo = sb("wr_lo", [P, E], F32R)
        br_sb = sb("br_sb", [P, E])

        x_ln = sb("x_ln", [P, TT, D])
        ctxT_in = sb("ctxT_in", [P, S])
        ln1_stats = sb("ln1_stats", [P, TT, 6])
        ln1_mv = sb("ln1_mv", [P, TT, 2])
        ln1_var = sb("ln1_var", [P, TT])
        ln1_rstd = sb("ln1_rstd", [P, TT])
        xn = sb("xn", [P, TT, D])
        xnT = sb("xnT", [P, S])
        q_parts = sb("q_parts", [P, 2, S], F32R)
        k_parts = sb("k_parts", [P, 2, S], F32R)
        k_stack = sb("k_stack", [P, PAIRS, S], F32R)
        q_stack = sb("q_stack", [P, PAIRS, 2, S], F32R)
        v_pad = sb("v_pad", [P, TT, H, 32])
        q_scratch = nc.dram_tensor("q_scratch", (P, 2, S), F32, kind="Internal").ap()
        k_scratch = nc.dram_tensor("k_scratch", (2, P, 2, S), F32, kind="Internal").ap()

        shift_m = sb("shift_m", [P, 2, P], F32R)
        e_sb = sb("e_sb", [P, 2, HQ])
        half_sum = sb("half_sum", [P, HQ // 2])
        quarter_sum = sb("quarter_sum", [P, HQ // 4])
        e_sum = sb("e_sum", [P, 2, P])
        log_sum = sb("log_sum", [P, 2, P])
        e_rcp = sb("e_rcp", [P, 2, P])
        attn = sb("attn", [P, TT, H, S])
        headsT = sb("headsT", [P, S])
        x_res = sb("x_res", [P, TT, D])
        x1 = sb("x1", [P, TT, D])

        ln2_stats = sb("ln2_stats", [P, TT, 6])
        ln2_mv = sb("ln2_mv", [P, TT, 2])
        ln2_var = sb("ln2_var", [P, TT])
        ln2_rstd = sb("ln2_rstd", [P, TT])
        x1n = sb("x1n", [P, TT, D])
        x1T_hi = sb("x1T_hi", [P, S], F32R)
        x1T_lo = sb("x1T_lo", [P, S], F32R)
        logits = sb("logits", [P, TT, E])
        top8 = sb("top8", [P, TT, 8])
        top8_at = sb("top8_at", [P, TT, 8], U32)
        top8_at_f = sb("top8_at_f", [P, TT, 8])
        rel = sb("rel", [P, TT, E])
        first = sb("first", [P, TT, E])
        second = sb("second", [P, TT, E])
        chosen = sb("chosen", [P, TT, E])
        rel_exp = sb("rel_exp", [P, TT, E])
        chosen_exp = sb("chosen_exp", [P, TT, E])
        gate_sum = sb("gate_sum", [P, TT])
        gate_rcp = sb("gate_rcp", [P, TT])
        gates = sb("gates", [P, TT, E])
        gatesT = sb("gatesT", [E, S])
        hT = sb("hT", [P, 2, HC, S])
        acc = sb("acc", [P, TT, D])

        score_ps = ps("score_ps", [P, 2, HQ])
        h_ps = ps("h_ps", [P, 2, HC * S])
        y_ps = ps("y_ps", [P, BANK])
        misc_ps = ps("misc_ps", [P, BANK])

        wq_in, w1_in, w2_in, small_in = sem("wq_in"), sem("w1_in"), sem("w2_in"), sem("small_in")
        x_ln_in, x_res_in, ctx_in = sem("x_ln_in"), sem("x_res_in"), sem("ctx_in")
        zeroed, ident_made, pool_made = sem("zeroed"), sem("ident_made"), sem("pool_made")
        neg_ident_made, parts_zeroed = sem("neg_ident_made"), sem("parts_zeroed")
        w1_hi_made, w1_lo_made, wr_hi_made, wr_lo_made = (
            sem("w1_hi_made"), sem("w1_lo_made"), sem("wr_hi_made"), sem("wr_lo_made"))
        ln1_step, ln1_var_made, ln1_rstd_made, xn_made = (
            sem("ln1_step"), sem("ln1_var_made"), sem("ln1_rstd_made"), sem("xn_made"))
        xnT_done, xnT_taken = sem("xnT_done"), sem("xnT_taken")
        q_done, q_hi_made, q_lo_made, q_spilled = (
            sem("q_done"), sem("q_hi_made"), sem("q_lo_made"), sem("q_spilled"))
        k_done, k_hi_made, k_lo_made, k_spilled = (
            sem("k_done"), sem("k_hi_made"), sem("k_lo_made"), sem("k_spilled"))
        stacks_in, v_done, v_taken = sem("stacks_in"), sem("v_done"), sem("v_taken")
        scores_done, max_made, shifted, exp_made = (
            sem("scores_done"), sem("max_made"), sem("shifted"), sem("exp_made"))
        sum_step, sum_made, log_made, rcp_made, attn_made = (
            sem("sum_step"), sem("sum_made"), sem("log_made"), sem("rcp_made"), sem("attn_made"))
        av_done, heads_taken, wo_done, x1_made = (
            sem("av_done"), sem("heads_taken"), sem("wo_done"), sem("x1_made"))
        ln2_step, ln2_var_made, ln2_rstd_made, x1n_made = (
            sem("ln2_step"), sem("ln2_var_made"), sem("ln2_rstd_made"), sem("x1n_made"))
        x1T_done, x1T_hi_made, x1T_lo_made = sem("x1T_done"), sem("x1T_hi_made"), sem("x1T_lo_made")
        router_done, logits_made, router_step, rel_made, rel_exp_made, gates_made = (
            sem("router_done"), sem("logits_made"), sem("router_step"), sem("rel_made"),
            sem("rel_exp_made"), sem("gates_made"))
        gatesT_done, gatesT_taken, b2_done, acc_begun = (
            sem("gatesT_done"), sem("gatesT_taken"), sem("b2_done"), sem("acc_begun"))
        h_done, relu_made, y_done, gated, stored = (
            sem("h_done"), sem("relu_made"), sem("y_done"), sem("gated"), sem("stored"))
        ROUTER_STEPS = 9

        def wait(eng, semaphore, n):
            if not (isinstance(n, int) and n <= 0):
                eng.wait_ge(semaphore, n)

        def pipeline(eng, step):
            step(0, True, True, False)
            with eng.Fori(1, B - 1) as i:
                step(i, True, True, True)
            step(B - 1, True, False, True)
            step(B, False, False, True)

        block = stack.enter_context(nc.Block())

        @block.sync
        def _(sp):
            def load_prepare(b):
                wait(sp, xn_made, b)
                sp.dma_start(x_ln[:], x[b].rearrange("(t p) d -> p t d", p=P)).then_inc(x_ln_in, 16)
                wait(sp, v_done, b)
                sp.dma_start(ctxT_in[:], ctx_t[b]).then_inc(ctx_in, 16)

            def load_residual(b):
                wait(sp, x1_made, b)
                sp.dma_start(x_res[:], x[b].rearrange("(t p) d -> p t d", p=P)).then_inc(x_res_in, 16)

            def restack(b):
                sp.wait_ge(q_hi_made, b + 1)
                sp.wait_ge(q_lo_made, b + 1)
                sp.dma_start(q_scratch, q_parts[:].bitcast(F32)).then_inc(q_spilled, 16)
                sp.wait_ge(k_hi_made, b + 1)
                sp.wait_ge(k_lo_made, b + 1)
                for part in range(2):
                    src = k_parts[:, part, :].bitcast(F32).unsqueeze(1).to_broadcast([P, 2, S])
                    sp.dma_start(k_scratch[part], src).then_inc(k_spilled, 16)
                if isinstance(b, int) and b == 0:
                    sp.wait_ge(parts_zeroed, 1)
                sp.wait_ge(q_spilled, 16 * (b + 1))
                for odd in range(2):
                    for copy in range(2):
                        row = 64 * odd + 32 * copy
                        src = q_scratch.rearrange("(j o d) c s -> o (d c) j s", o=2, d=DH)[odd]
                        sp.dma_start(q_stack[row:row + 32, :, odd, :].bitcast(F32), src).then_inc(stacks_in, 16)
                sp.wait_ge(k_spilled, 32 * (b + 1))
                for odd in range(2):
                    for copy in range(2):
                        row = 64 * odd + 32 * copy
                        src = k_scratch[copy].rearrange("(j o d) c s -> o (d c) j s", o=2, d=DH)[odd]
                        sp.dma_start(k_stack[row:row + 32, :, :].bitcast(F32), src).then_inc(stacks_in, 16)

            def store(b):
                sp.wait_ge(gated, E * (b + 1))
                sp.dma_start(out[b].rearrange("(t p) d -> p t d", p=P), acc[:]).then_inc(stored, 16)

            def step(i, attend, prepare, experts):
                if prepare:
                    load_prepare(i + 1)
                if attend:
                    load_residual(i)
                if prepare:
                    restack(i + 1)
                if experts:
                    store(i - 1)

            sp.dma_start(x_ln[:], x[0].rearrange("(t p) d -> p t d", p=P)).then_inc(x_ln_in, 16)
            sp.dma_start(w_qkvo[:], w_attn).then_inc(wq_in, 16)
            sp.dma_start(ctxT_in[:], ctx_t[0]).then_inc(ctx_in, 16)
            sp.dma_start(wr_sb[:], wr).then_inc(small_in, 16)
            sp.dma_start(br_sb[:], br.unsqueeze(0).to_broadcast([P, E])).then_inc(small_in, 16)
            sp.dma_start(b1_sb[:], b1_t).then_inc(small_in, 16)
            sp.dma_start(b2_sb[:], b2).then_inc(small_in, 16)
            sp.dma_start(w1_sb[:], w1.rearrange("e d h -> d e h")).then_inc(w1_in, 16)
            sp.dma_start(w2_sb[:], w2.rearrange("e (c p) d -> p (e c) d", p=P)).then_inc(w2_in, 16)
            restack(0)
            pipeline(sp, step)
            sp.wait_ge(stored, 16 * B)

        @block.tensor
        def _(pe):
            def transpose_xn(b, experts):
                pe.wait_ge(xn_made, b + 1)
                if experts:
                    pe.wait_ge(acc_begun, b - 1)
                for t in range(TT):
                    mm = nc.tensor.transpose(misc_ps[:, t * P:(t + 1) * P], xn[:, t, :], ident[:])
                mm.then_inc(xnT_done, 1)

            def project_q(b):
                pe.wait_ge(xnT_taken, b + 1)
                nc.tensor.matmul(misc_ps[:, 0:S], w_qkvo[:, 0, :], xnT[:], start=True, stop=True).then_inc(q_done, 1)

            def project_k(b):
                pe.wait_ge(ctx_in, 16 * (b + 1))
                pe.wait_ge(q_hi_made, b + 1)
                pe.wait_ge(q_lo_made, b + 1)
                nc.tensor.matmul(misc_ps[:, 0:S], w_qkvo[:, 1, :], ctxT_in[:], start=True, stop=True).then_inc(k_done, 1)

            def project_v(b):
                wait(pe, heads_taken, b)
                if isinstance(b, int) and b == 0:
                    pe.wait_ge(k_hi_made, 1)
                    pe.wait_ge(k_lo_made, 1)
                for t in range(TT):
                    mm = nc.tensor.matmul(misc_ps[:, t * P:(t + 1) * P], ctxT_in[:, t * P:(t + 1) * P],
                                          w_qkvo[:, 2, :], start=True, stop=True)
                mm.then_inc(v_done, 1)

            def scores(b, u):
                n, kt, qt = UNITS * b + u, u // TT, u % TT
                if u == 0:
                    pe.wait_ge(stacks_in, 16 * STACK_READS * (b + 1))
                wait(pe, exp_made, n - 1)
                for j in range(PAIRS):
                    mm = nc.tensor.matmul(
                        score_ps[:, u % 2, 2 * j * P:(2 * j + 2) * P], k_stack[:, j, kt * P:(kt + 1) * P],
                        q_stack[:, j, :, qt * P:(qt + 1) * P], start=(j % 2 == 0), stop=True,
                        skip_group_check=True)
                mm.then_inc(scores_done, 1)

            def subtract_max(b, u):
                pe.wait_ge(max_made, UNITS * b + u + 1)
                m4 = shift_m[:, u % 2, :].unsqueeze(1).to_broadcast([P, BANK // P, P])
                for half in range(2):
                    mm = nc.tensor.matmul(score_ps[:, u % 2, half * BANK:(half + 1) * BANK], neg_ident[:], m4,
                                          start=False, stop=True, skip_group_check=True)
                mm.then_inc(shifted, 1)

            def attend_values(b, prepare):
                pe.wait_ge(attn_made, UNITS * (b + 1))
                pe.wait_ge(v_taken, b + 1)
                if prepare:
                    pe.wait_ge(k_hi_made, b + 2)
                    pe.wait_ge(k_lo_made, b + 2)
                else:
                    pe.wait_ge(acc_begun, b)
                for odd in range(2):
                    for kt in range(TT):
                        for g in range(PAIRS):
                            h = 2 * g + odd
                            mm = nc.tensor.matmul(misc_ps[32 * g:32 * g + 32, 0:S], v_pad[:, kt, h, :],
                                                  attn[:, kt, h, :], start=(odd == 0 and kt == 0),
                                                  stop=(odd == 1 and kt == TT - 1))
                mm.then_inc(av_done, 1)

            def project_out(b, prepare):
                pe.wait_ge(heads_taken, b + 1)
                if prepare:
                    pe.wait_ge(v_taken, b + 2)
                for t in range(TT):
                    mm = nc.tensor.matmul(misc_ps[:, t * P:(t + 1) * P], headsT[:, t * P:(t + 1) * P],
                                          w_qkvo[:, 3, :], start=True, stop=True)
                mm.then_inc(wo_done, 1)

            def transpose_x1n(b):
                pe.wait_ge(x1n_made, b + 1)
                for t in range(TT):
                    mm = nc.tensor.transpose(misc_ps[:, t * P:(t + 1) * P], x1n[:, t, :], ident[:])
                mm.then_inc(x1T_done, 1)

            def route(b):
                pe.wait_ge(x1T_hi_made, b + 1)
                pe.wait_ge(x1T_lo_made, b + 1)
                if isinstance(b, int) and b == 0:
                    pe.wait_ge(wr_hi_made, 1)
                    pe.wait_ge(wr_lo_made, 1)
                for t in range(TT):
                    for n, (xt, w) in enumerate(((x1T_lo, wr_lo), (x1T_lo, wr_hi), (x1T_hi, wr_lo), (x1T_hi, wr_hi))):
                        mm = nc.tensor.matmul(misc_ps[:, t * E:(t + 1) * E], xt[:, t * P:(t + 1) * P], w[:],
                                              start=(n == 0), stop=(n == 3))
                mm.then_inc(router_done, 1)

            def transpose_gates(b):
                pe.wait_ge(gates_made, b + 1)
                for t in range(TT):
                    mm = nc.tensor.transpose(misc_ps[0:E, t * P:(t + 1) * P], gates[:, t, :], ident[:])
                mm.then_inc(gatesT_done, 1)

            def gated_b2(b):
                pe.wait_ge(gatesT_taken, b + 1)
                for t in range(TT):
                    mm = nc.tensor.matmul(misc_ps[:, t * P:(t + 1) * P], gatesT[:, t * P:(t + 1) * P], b2_sb[:],
                                          start=True, stop=True)
                mm.then_inc(b2_done, 1)

            def expert_up(b, e):
                n = E * b + e
                if e == 0 and isinstance(b, int) and b == 0:
                    pe.wait_ge(w1_hi_made, 1)
                    pe.wait_ge(w1_lo_made, 1)
                wait(pe, relu_made, n if e == 0 else n - 1)
                for c in range(HC):
                    for k, (w, xt) in enumerate(((w1_lo, x1T_hi), (w1_hi, x1T_lo), (w1_hi, x1T_hi))):
                        mm = nc.tensor.matmul(h_ps[:, e % 2, c * S:(c + 1) * S], w[:, e, c * P:(c + 1) * P], xt[:],
                                              start=(k == 0), stop=(k == 2))
                mm.then_inc(h_done, 1)

            def expert_down(b, e):
                n = E * b + e
                pe.wait_ge(relu_made, n + 1)
                wait(pe, gated, n)
                for t in range(TT):
                    for c in range(HC):
                        mm = nc.tensor.matmul(y_ps[:, t * D:(t + 1) * D], hT[:, e % 2, c, t * P:(t + 1) * P],
                                              w2_sb[:, e * HC + c, :], start=(c == 0), stop=(c == HC - 1))
                mm.then_inc(y_done, 1)

            def step(i, attend, prepare, experts):
                f = i - 1
                if attend:
                    scores(i, 0)
                    scores(i, 1)
                if experts:
                    transpose_x1n(f)
                if attend:
                    subtract_max(i, 0)
                if experts:
                    route(f)
                    expert_up(f, 0)
                if attend:
                    subtract_max(i, 1)
                if experts:
                    expert_up(f, 1)
                if attend:
                    scores(i, 2)
                if experts:
                    transpose_gates(f)
                    expert_down(f, 0)
                    expert_up(f, 2)
                    gated_b2(f)
                if attend:
                    subtract_max(i, 2)
                if experts:
                    expert_down(f, 1)
                    expert_up(f, 3)
                if attend:
                    scores(i, 3)
                if prepare:
                    transpose_xn(i + 1, experts)
                if experts:
                    expert_down(f, 2)
                    expert_up(f, 4)
                if attend:
                    subtract_max(i, 3)
                if prepare:
                    project_q(i + 1)
                if experts:
                    expert_down(f, 3)
                    expert_up(f, 5)
                if prepare:
                    project_k(i + 1)
                if experts:
                    expert_down(f, 4)
                    expert_up(f, 6)
                    expert_down(f, 5)
                if attend:
                    attend_values(i, prepare)
                if experts:
                    expert_up(f, 7)
                if prepare:
                    project_v(i + 1)
                if experts:
                    expert_down(f, 6)
                if attend:
                    project_out(i, prepare)
                if experts:
                    expert_down(f, 7)

            pe.wait_ge(ident_made, 1)
            pe.wait_ge(wq_in, 16)
            transpose_xn(0, False)
            project_q(0)
            project_k(0)
            project_v(0)
            pe.wait_ge(neg_ident_made, 1)
            pe.wait_ge(w2_in, 16)
            pe.wait_ge(small_in, 64)
            pipeline(pe, step)

        @block.scalar
        def _(act):
            def take(dst, src, done, b, made):
                act.wait_ge(done, b + 1)
                nc.scalar.activation(dst, src, ACT.Copy).then_inc(made, 1)

            def take_xnT(b):
                wait(act, q_done, b)
                take(xnT[:], misc_ps[:, 0:S], xnT_done, b, xnT_taken)

            def take_q_hi(b):
                wait(act, q_spilled, 16 * b)
                take(q_parts[:, 0, :], misc_ps[:, 0:S], q_done, b, q_hi_made)

            def take_k_hi(b):
                wait(act, k_spilled, 32 * b)
                take(k_parts[:, 0, :], misc_ps[:, 0:S], k_done, b, k_hi_made)

            def take_v(b):
                wait(act, av_done, b)
                if isinstance(b, int) and b == 0:
                    act.wait_ge(parts_zeroed, 2)
                dst = v_pad[:].rearrange("p k (j o) (a d) -> p (k j) (o a) d", o=2, d=DH)[:, :, 0:4:3, :]
                take(dst, misc_ps[:, 0:S].rearrange("p (n o d) -> p n o d", o=2, d=DH), v_done, b, v_taken)

            def exponentiate(b, u):
                n = UNITS * b + u
                act.wait_ge(shifted, n + 1)
                wait(act, attn_made, n - 1)
                nc.scalar.activation(e_sb[:, u % 2, :], score_ps[:, u % 2, :], ACT.Exp, scale=SCALE).then_inc(exp_made, 1)

            def invert_sum(b, u):
                n = UNITS * b + u
                act.wait_ge(sum_made, n + 1)
                nc.scalar.activation(log_sum[:, u % 2, :], e_sum[:, u % 2, :], ACT.Ln).then_inc(log_made, 1)
                act.wait_ge(log_made, n + 1)
                nc.scalar.activation(e_rcp[:, u % 2, :], log_sum[:, u % 2, :], ACT.Exp, scale=-1.0).then_inc(rcp_made, 1)

            def take_heads(b):
                wait(act, wo_done, b)
                take(headsT[:], misc_ps[:, 0:S], av_done, b, heads_taken)

            def take_x1T_hi(b):
                wait(act, h_done, E * b)
                take(x1T_hi[:], misc_ps[:, 0:S], x1T_done, b, x1T_hi_made)

            def router_exp(b):
                act.wait_ge(rel_made, b + 1)
                nc.scalar.activation(rel_exp[:], rel[:], ACT.Exp).then_inc(rel_exp_made, 1)

            def take_gatesT(b):
                wait(act, b2_done, b)
                take(gatesT[:], misc_ps[0:E, 0:S], gatesT_done, b, gatesT_taken)

            def relu(b, e):
                n = E * b + e
                act.wait_ge(h_done, n + 1)
                wait(act, y_done, n if e == 0 else n - 1)
                for c in range(HC):
                    op = nc.scalar.activation(hT[:, e % 2, c, :], h_ps[:, e % 2, c * S:(c + 1) * S], ACT.Relu,
                                              bias=b1_sb[:, e * HC + c:e * HC + c + 1])
                op.then_inc(relu_made, 1)

            def step(i, attend, prepare, experts):
                f = i - 1
                if experts:
                    take_x1T_hi(f)
                if attend:
                    exponentiate(i, 0)
                if experts:
                    relu(f, 0)
                if attend:
                    exponentiate(i, 1)
                if experts:
                    relu(f, 1)
                if attend:
                    invert_sum(i, 0)
                if experts:
                    router_exp(f)
                    take_gatesT(f)
                    relu(f, 2)
                if attend:
                    invert_sum(i, 1)
                    exponentiate(i, 2)
                if experts:
                    relu(f, 3)
                if prepare:
                    take_xnT(i + 1)
                if experts:
                    relu(f, 4)
                if attend:
                    invert_sum(i, 2)
                    exponentiate(i, 3)
                if prepare:
                    take_q_hi(i + 1)
                if experts:
                    relu(f, 5)
                if attend:
                    invert_sum(i, 3)
                if prepare:
                    take_k_hi(i + 1)
                if experts:
                    relu(f, 6)
                if attend:
                    take_heads(i)
                if experts:
                    relu(f, 7)
                if prepare:
                    take_v(i + 1)

            nc.scalar.preload_act_table_set("natural_log_exp_and_others")
            act.wait_ge(small_in, 64)
            take_xnT(0)
            take_q_hi(0)
            take_k_hi(0)
            take_v(0)
            pipeline(act, step)

        @block.vector
        def _(dve):
            def norm_stats(src, stats, step_sem):
                for t in range(TT):
                    op = nc.vector.bn_stats(stats[:, t, :], src[:, t, :])
                op.then_inc(step_sem, 1)

            def norm_var(b, stats, mv, var, step_sem, var_made):
                for t in range(TT):
                    op = nc.vector.bn_aggr(mv[:, t, :], stats[:, t, :])
                op.then_inc(step_sem, 1)
                dve.wait_ge(step_sem, 2 * b + 2)
                nc.vector.tensor_scalar(var[:], mv[:, :, 1], EPS, None, ALU.add).then_inc(var_made, 1)

            def norm_apply(src, mv, rstd, dst, made):
                for t in range(TT):
                    op = nc.vector.tensor_scalar(dst[:, t, :], src[:, t, :], mv[:, t, 0:1], rstd[:, t:t + 1],
                                                 ALU.subtract, ALU.mult)
                op.then_inc(made, 1)

            def ln1_begin(b):
                dve.wait_ge(x_ln_in, 16 * (b + 1))
                norm_stats(x_ln, ln1_stats, ln1_step)

            def ln1_end(b):
                dve.wait_ge(ln1_rstd_made, b + 1)
                wait(dve, xnT_done, b)
                norm_apply(x_ln, ln1_mv, ln1_rstd, xn, xn_made)

            def ln2_begin(b):
                dve.wait_ge(wo_done, b + 1)
                dve.wait_ge(x_res_in, 16 * (b + 1))
                wait(dve, acc_begun, b)
                nc.vector.tensor_tensor(x1[:].rearrange("p t d -> p (t d)"), misc_ps[:, 0:S],
                                        x_res[:].rearrange("p t d -> p (t d)"), ALU.add).then_inc(x1_made, 1)
                dve.wait_ge(x1_made, b + 1)
                norm_stats(x1, ln2_stats, ln2_step)

            def ln2_end(b):
                dve.wait_ge(ln2_rstd_made, b + 1)
                wait(dve, x1T_done, b)
                norm_apply(x1, ln2_mv, ln2_rstd, x1n, x1n_made)

            def low_part(dst, hi, hi_made, b, made):
                dve.wait_ge(hi_made, b + 1)
                nc.vector.tensor_tensor(dst, misc_ps[:, 0:S], hi.bitcast(F32), ALU.subtract).then_inc(made, 1)

            def q_lo(b):
                low_part(q_parts[:, 1, :], q_parts[:, 0, :], q_hi_made, b, q_lo_made)

            def k_lo(b):
                low_part(k_parts[:, 1, :], k_parts[:, 0, :], k_hi_made, b, k_lo_made)

            def x1T_low(b):
                wait(dve, h_done, E * b)
                low_part(x1T_lo[:], x1T_hi[:], x1T_hi_made, b, x1T_lo_made)

            def head_max(b, u):
                dve.wait_ge(scores_done, UNITS * b + u + 1)
                nc.vector.tensor_reduce(shift_m[:, u % 2, :], score_ps[:, u % 2, :].rearrange("p (h q) -> p q h", h=H),
                                        AX.X, ALU.max).then_inc(max_made, 1)

            def normalize(b, u):
                kt, qt = u // TT, u % TT
                dve.wait_ge(rcp_made, UNITS * b + u + 1)
                if u == 0:
                    wait(dve, av_done, b)
                nc.vector.tensor_tensor(attn[:, kt, :, qt * P:(qt + 1) * P],
                                        e_sb[:, u % 2, :].rearrange("p (h q) -> p h q", h=H),
                                        e_rcp[:, u % 2, :].unsqueeze(1).to_broadcast([P, H, P]),
                                        ALU.mult).then_inc(attn_made, 1)

            def take_logits(b):
                dve.wait_ge(router_done, b + 1)
                nc.vector.tensor_tensor(logits[:], misc_ps[:, 0:TT * E].rearrange("p (t e) -> p t e", e=E),
                                        br_sb[:].unsqueeze(1).to_broadcast([P, TT, E]), ALU.add).then_inc(logits_made, 1)

            def choose_experts(b):
                at = ROUTER_STEPS * b
                for t in range(TT):
                    op = nc.vector.max(top8[:, t, :], logits[:, t, :])
                op.then_inc(router_step, 1)
                dve.wait_ge(router_step, at + 1)
                nc.vector.tensor_tensor(rel[:], logits[:], top8[:, :, 0:1].to_broadcast([P, TT, E]),
                                        ALU.subtract).then_inc(rel_made, 1)
                for t in range(TT):
                    op = nc.vector.max_index(top8_at[:, t, :], top8[:, t, :], logits[:, t, :])
                op.then_inc(router_step, 1)
                dve.wait_ge(router_step, at + 2)
                nc.vector.tensor_copy(top8_at_f[:], top8_at[:]).then_inc(router_step, 1)
                dve.wait_ge(router_step, at + 3)
                for n, place in enumerate((first, second)):
                    nc.vector.tensor_tensor(place[:], iota8[:].unsqueeze(1).to_broadcast([P, TT, E]),
                                            top8_at_f[:, :, n:n + 1].to_broadcast([P, TT, E]),
                                            ALU.is_equal).then_inc(router_step, 1)
                dve.wait_ge(router_step, at + 5)
                nc.vector.tensor_tensor(chosen[:], first[:], second[:], ALU.add).then_inc(router_step, 1)

            def make_gates(b):
                at = ROUTER_STEPS * b
                dve.wait_ge(rel_exp_made, b + 1)
                dve.wait_ge(router_step, at + 6)
                nc.vector.tensor_tensor(chosen_exp[:], rel_exp[:], chosen[:], ALU.mult).then_inc(router_step, 1)
                dve.wait_ge(router_step, at + 7)
                nc.vector.tensor_reduce(gate_sum[:], chosen_exp[:], AX.X, ALU.add).then_inc(router_step, 1)
                dve.wait_ge(router_step, at + 8)
                nc.vector.reciprocal(gate_rcp[:], gate_sum[:]).then_inc(router_step, 1)
                dve.wait_ge(router_step, at + 9)
                nc.vector.tensor_tensor(gates[:], chosen_exp[:], gate_rcp[:].unsqueeze(2).to_broadcast([P, TT, E]),
                                        ALU.mult).then_inc(gates_made, 1)

            def begin_acc(b):
                dve.wait_ge(b2_done, b + 1)
                wait(dve, stored, 16 * b)
                nc.vector.tensor_tensor(acc[:].rearrange("p t d -> p (t d)"), misc_ps[:, 0:S],
                                        x1[:].rearrange("p t d -> p (t d)"), ALU.add).then_inc(acc_begun, 1)

            def add_expert(b, e):
                n = E * b + e
                dve.wait_ge(y_done, n + 1)
                if e == 0:
                    dve.wait_ge(acc_begun, b + 1)
                wait(dve, gated, n)
                for t in range(TT):
                    op = nc.vector.scalar_tensor_tensor(out=acc[:, t, :], in0=y_ps[:, t * D:(t + 1) * D],
                                                        scalar=gates[:, t, e:e + 1], in1=acc[:, t, :],
                                                        op0=ALU.mult, op1=ALU.add)
                op.then_inc(gated, 1)

            def step(i, attend, prepare, experts):
                f = i - 1
                if attend:
                    head_max(i, 0)
                if experts:
                    x1T_low(f)
                if experts:
                    take_logits(f)
                    dve.wait_ge(logits_made, f + 1)
                if attend:
                    head_max(i, 1)
                if experts:
                    choose_experts(f)
                if attend:
                    normalize(i, 0)
                if experts:
                    make_gates(f)
                if attend:
                    head_max(i, 2)
                if experts:
                    begin_acc(f)
                if prepare:
                    ln1_begin(i + 1)
                    dve.wait_ge(ln1_step, 2 * i + 3)
                if experts:
                    add_expert(f, 0)
                if prepare:
                    norm_var(i + 1, ln1_stats, ln1_mv, ln1_var, ln1_step, ln1_var_made)
                if attend:
                    normalize(i, 1)
                if experts:
                    add_expert(f, 1)
                if attend:
                    head_max(i, 3)
                if prepare:
                    ln1_end(i + 1)
                if experts:
                    add_expert(f, 2)
                if attend:
                    normalize(i, 2)
                if experts:
                    add_expert(f, 3)
                if prepare:
                    q_lo(i + 1)
                if experts:
                    add_expert(f, 4)
                if attend:
                    normalize(i, 3)
                if prepare:
                    k_lo(i + 1)
                if experts:
                    add_expert(f, 5)
                    add_expert(f, 6)
                if attend:
                    ln2_begin(i)
                    dve.wait_ge(ln2_step, 2 * i + 1)
                if experts:
                    add_expert(f, 7)
                if attend:
                    norm_var(i, ln2_stats, ln2_mv, ln2_var, ln2_step, ln2_var_made)
                    ln2_end(i)

            ln1_begin(0)
            dve.wait_ge(ln1_step, 1)
            norm_var(0, ln1_stats, ln1_mv, ln1_var, ln1_step, ln1_var_made)
            nc.vector.memset(q_stack[:].bitcast(F32), 0.0).then_inc(parts_zeroed, 1)
            nc.vector.memset(v_pad[:], 0.0).then_inc(parts_zeroed, 1)
            ln1_end(0)
            dve.wait_ge(ident_made, 1)
            nc.vector.tensor_scalar(neg_ident[:], ident[:], -1.0, None, ALU.mult).then_inc(neg_ident_made, 1)
            q_lo(0)
            k_lo(0)
            dve.wait_ge(small_in, 64)
            nc.vector.tensor_copy(wr_hi[:], wr_sb[:]).then_inc(wr_hi_made, 1)
            dve.wait_ge(wr_hi_made, 1)
            nc.vector.tensor_tensor(wr_lo[:], wr_sb[:], wr_hi[:].bitcast(F32), ALU.subtract).then_inc(wr_lo_made, 1)
            dve.wait_ge(w1_in, 16)
            nc.vector.tensor_copy(w1_hi[:], w1_sb[:]).then_inc(w1_hi_made, 1)
            dve.wait_ge(pool_made, 1)
            pipeline(dve, step)

        @block.gpsimd
        def _(pool):
            def rstd(b, var, var_made, dst, made):
                pool.wait_ge(var_made, b + 1)
                nc.gpsimd.tensor_tensor(dst[:], var[:], neg_half[:], ALU.pow).then_inc(made, 1)

            def head_sum(b, u):
                n = UNITS * b + u
                pool.wait_ge(exp_made, n + 1)
                e = e_sb[:, u % 2, :]
                nc.gpsimd.tensor_tensor(half_sum[:], e[:, 0:HQ // 2], e[:, HQ // 2:HQ], ALU.add).then_inc(sum_step, 1)
                pool.wait_ge(sum_step, 2 * n + 1)
                nc.gpsimd.tensor_tensor(quarter_sum[:], half_sum[:, 0:HQ // 4], half_sum[:, HQ // 4:HQ // 2],
                                        ALU.add).then_inc(sum_step, 1)
                pool.wait_ge(sum_step, 2 * n + 2)
                nc.gpsimd.tensor_tensor(e_sum[:, u % 2, :], quarter_sum[:, 0:P], quarter_sum[:, P:2 * P],
                                        ALU.add).then_inc(sum_made, 1)

            def step(i, attend, prepare, experts):
                if attend:
                    head_sum(i, 0)
                    head_sum(i, 1)
                if prepare:
                    rstd(i + 1, ln1_var, ln1_var_made, ln1_rstd, ln1_rstd_made)
                if attend:
                    head_sum(i, 2)
                    head_sum(i, 3)
                    rstd(i, ln2_var, ln2_var_made, ln2_rstd, ln2_rstd_made)

            nc.gpsimd.memset(neg_half[:], -0.5).then_inc(zeroed, 1)
            nc.gpsimd.memset(ident[:], 0.0).then_inc(zeroed, 1)
            pool.wait_ge(zeroed, 2)
            nc.gpsimd.affine_select(out=ident[:], in_=ident[:], compare_op=ALU.not_equal, fill=1.0, base=0,
                                    pattern=[[-1, P]], channel_multiplier=1).then_inc(ident_made, 1)
            rstd(0, ln1_var, ln1_var_made, ln1_rstd, ln1_rstd_made)
            for e in range(E):
                op = nc.gpsimd.memset(iota8[:, e:e + 1], float(e))
            op.then_inc(pool_made, 1)
            pool.wait_ge(w1_hi_made, 1)
            nc.gpsimd.tensor_tensor(w1_lo[:], w1_sb[:], w1_hi[:].bitcast(F32), ALU.subtract).then_inc(w1_lo_made, 1)
            pipeline(pool, step)


def kernel(x, ctx_1024, L0_xattn_W_Q, L0_xattn_W_K, L0_xattn_W_V, L0_xattn_W_O, L0_ffn_Wr, L0_ffn_br,
           L0_ffn_W1, L0_ffn_b1, L0_ffn_W2, L0_ffn_b2):
    import numpy as np
    import concourse.bacc as bacc
    from concourse.bass_utils import run_bass_kernel_spmd

    E, HID = L0_ffn_b1.shape
    w_attn = np.stack([np.asarray(w).T for w in (L0_xattn_W_Q, L0_xattn_W_K, L0_xattn_W_V, L0_xattn_W_O)], axis=1)
    given = {
        "x": x,
        "ctx_t": np.asarray(ctx_1024).transpose(0, 2, 1),
        "w_attn": w_attn,
        "wr": L0_ffn_Wr,
        "br": L0_ffn_br,
        "w1": L0_ffn_W1,
        "b1_t": np.asarray(L0_ffn_b1).reshape(E * HID // P, P).T,
        "w2": L0_ffn_W2,
        "b2": L0_ffn_b2,
    }
    nc = bacc.Bacc("TRN2", target_bir_lowering=False, num_devices=1)
    arrays, args = {}, []
    for name, a in given.items():
        a = np.ascontiguousarray(a)
        arrays[f"in_{name}"] = a
        args.append(nc.dram_tensor(f"in_{name}", a.shape, mybir.dt.from_np(a.dtype), kind="ExternalInput").ap())
    shape = tuple(np.asarray(x).shape)
    args.append(nc.dram_tensor("out_y", shape, F32, kind="ExternalOutput").ap())
    build(nc, *args)
    r = run_bass_kernel_spmd(nc, [arrays], core_ids=[0])
    return r.results[0]["out_y"]
```

```python
from contextlib import ExitStack

import concourse.bass as bass
from concourse import mybir

F32 = mybir.dt.float32
F32R = mybir.dt.float32r
U32 = mybir.dt.uint32
ALU = mybir.AluOpType
ACT = mybir.ActivationFunctionType
AX = mybir.AxisListType

P = 128
EPS = 1e-5


def build(nc, x, ctx_t, w_attn, wr, br, w1, b1_t, w2, b2, out):
    B, S, D = x.shape
    H, DH = 8, D // 8
    E, HID = w1.shape[0], w1.shape[2]
    TT = S // P
    HC = HID // P
    PAIRS = H // 2
    UNITS = TT * TT
    HQ = H * P
    BANK = 512
    SCALE = float(DH) ** -0.5
    assert D == P and S == 256 and UNITS == 4

    with ExitStack() as stack:
        def sb(name, shape, dt=F32):
            return stack.enter_context(nc.sbuf_tensor(name, shape, dt))

        def ps(name, shape, dt=F32):
            return stack.enter_context(nc.psum_tensor(name, shape, dt))

        def sem(name):
            return stack.enter_context(nc.semaphore(name))

        ident = sb("ident", [P, P])
        neg_ident = sb("neg_ident", [P, P], F32R)
        iota8 = sb("iota8", [P, E])
        neg_half = sb("neg_half", [P, TT])
        w_qkvo = sb("w_qkvo", [P, 4, D])
        w1_sb = sb("w1_sb", [P, E, HID])
        w1_hi = sb("w1_hi", [P, E, HID], F32R)
        w1_lo = sb("w1_lo", [P, E, HID], F32R)
        b1_sb = sb("b1_sb", [P, E * HC])
        w2_sb = sb("w2_sb", [P, E * HC, D])
        b2_sb = sb("b2_sb", [E, D])
        wr_sb = sb("wr_sb", [P, E])
        wr_hi = sb("wr_hi", [P, E], F32R)
        wr_lo = sb("wr_lo", [P, E], F32R)
        br_sb = sb("br_sb", [P, E])

        x_ln = sb("x_ln", [P, TT, D])
        ctxT_in = sb("ctxT_in", [P, S])
        ln1_stats = sb("ln1_stats", [P, TT, 6])
        ln1_mv = sb("ln1_mv", [P, TT, 2])
        ln1_var = sb("ln1_var", [P, TT])
        ln1_rstd = sb("ln1_rstd", [P, TT])
        xn = sb("xn", [P, TT, D])
        xnT = sb("xnT", [P, S])
        q_parts = sb("q_parts", [P, 2, S], F32R)
        k_parts = sb("k_parts", [P, 2, S], F32R)
        k_stack = sb("k_stack", [P, PAIRS, S], F32R)
        q_stack = sb("q_stack", [P, PAIRS, 2, S], F32R)
        v_pad = sb("v_pad", [P, TT, H, 32])
        q_scratch = nc.dram_tensor("q_scratch", (P, 2, S), F32, kind="Internal").ap()
        k_scratch = nc.dram_tensor("k_scratch", (2, P, 2, S), F32, kind="Internal").ap()

        shift_m = sb("shift_m", [P, 2, P], F32R)
        e_sb = sb("e_sb", [P, UNITS, HQ])
        half_sum = sb("half_sum", [P, HQ // 2])
        quarter_sum = sb("quarter_sum", [P, HQ // 4])
        e_sum = sb("e_sum", [P, UNITS, P])
        log_sum = sb("log_sum", [P, UNITS, P])
        e_rcp = sb("e_rcp", [P, UNITS, P])
        attn = sb("attn", [P, TT, H, S])
        headsT = sb("headsT", [P, S])
        x_res = sb("x_res", [P, TT, D])
        x1 = sb("x1", [P, TT, D])

        ln2_stats = sb("ln2_stats", [P, TT, 6])
        ln2_mv = sb("ln2_mv", [P, TT, 2])
        ln2_var = sb("ln2_var", [P, TT])
        ln2_rstd = sb("ln2_rstd", [P, TT])
        x1n = sb("x1n", [P, TT, D])
        x1T_hi = sb("x1T_hi", [P, S], F32R)
        x1T_lo = sb("x1T_lo", [P, S], F32R)
        logits = sb("logits", [P, TT, E])
        top8 = sb("top8", [P, TT, 8])
        top8_at = sb("top8_at", [P, TT, 8], U32)
        top8_at_f = sb("top8_at_f", [P, TT, 8])
        rel = sb("rel", [P, TT, E])
        first = sb("first", [P, TT, E])
        second = sb("second", [P, TT, E])
        chosen = sb("chosen", [P, TT, E])
        rel_exp = sb("rel_exp", [P, TT, E])
        chosen_exp = sb("chosen_exp", [P, TT, E])
        gate_sum = sb("gate_sum", [P, TT])
        gate_rcp = sb("gate_rcp", [P, TT])
        gates = sb("gates", [P, TT, E])
        gatesT = sb("gatesT", [E, S])
        hT = sb("hT", [P, 2, HC, S])
        acc = sb("acc", [P, TT, D])
        y_out = sb("y_out", [P, TT, D])

        score_ps = ps("score_ps", [P, 2, HQ])
        h_ps = ps("h_ps", [P, HC * S])
        y_ps = ps("y_ps", [P, 2, BANK])
        misc_ps = ps("misc_ps", [P, BANK])

        wq_in, w1_in, w2_in, small_in = sem("wq_in"), sem("w1_in"), sem("w2_in"), sem("small_in")
        x_ln_in, x_res_in, ctx_in = sem("x_ln_in"), sem("x_res_in"), sem("ctx_in")
        zeroed, ident_made, pool_made = sem("zeroed"), sem("ident_made"), sem("pool_made")
        neg_ident_made, v_zeroed, stacks_free = sem("neg_ident_made"), sem("v_zeroed"), sem("stacks_free")
        w1_hi_made, w1_lo_made, wr_hi_made, wr_lo_made = (
            sem("w1_hi_made"), sem("w1_lo_made"), sem("wr_hi_made"), sem("wr_lo_made"))
        ln1_step, ln1_var_made, ln1_rstd_made, xn_made = (
            sem("ln1_step"), sem("ln1_var_made"), sem("ln1_rstd_made"), sem("xn_made"))
        xnT_done, xnT_taken = sem("xnT_done"), sem("xnT_taken")
        q_done, q_hi_made, q_lo_made, q_spilled = (
            sem("q_done"), sem("q_hi_made"), sem("q_lo_made"), sem("q_spilled"))
        k_done, k_hi_made, k_lo_made, k_spilled = (
            sem("k_done"), sem("k_hi_made"), sem("k_lo_made"), sem("k_spilled"))
        k_spilled2, k_stack_in, q_stack_in = sem("k_spilled2"), sem("k_stack_in"), sem("q_stack_in")
        v_done, v_taken = sem("v_done"), sem("v_taken")
        scores_done, max_made, shifted, exp_made = (
            sem("scores_done"), sem("max_made"), sem("shifted"), sem("exp_made"))
        sum_step, sum_made, log_made, rcp_made, attn_made = (
            sem("sum_step"), sem("sum_made"), sem("log_made"), sem("rcp_made"), sem("attn_made"))
        av_done, heads_taken, wo_done, x1_made = (
            sem("av_done"), sem("heads_taken"), sem("wo_done"), sem("x1_made"))
        ln2_step, ln2_var_made, ln2_rstd_made, x1n_made = (
            sem("ln2_step"), sem("ln2_var_made"), sem("ln2_rstd_made"), sem("x1n_made"))
        x1T_done, x1T_hi_made, x1T_lo_made = sem("x1T_done"), sem("x1T_hi_made"), sem("x1T_lo_made")
        router_done, logits_made, router_step, rel_made, rel_exp_made, gates_made = (
            sem("router_done"), sem("logits_made"), sem("router_step"), sem("rel_made"),
            sem("rel_exp_made"), sem("gates_made"))
        gatesT_done, gatesT_taken, b2_done, b2_added = (
            sem("gatesT_done"), sem("gatesT_taken"), sem("b2_done"), sem("b2_added"))
        h_done, relu_made, y_done, gated, stored = (
            sem("h_done"), sem("relu_made"), sem("y_done"), sem("gated"), sem("stored"))
        ROUTER_STEPS = 9
        B2_AFTER = 2

        def wait(eng, semaphore, n):
            if not (isinstance(n, int) and n <= 0):
                eng.wait_ge(semaphore, n)

        def pipeline(eng, step):
            step(0, True, True, False, False)
            step(1, True, True, True, False)
            with eng.Fori(2, B - 1) as i:
                step(i, True, True, True, True)
            step(B - 1, True, False, True, True)
            step(B, False, False, True, True)
            step(B + 1, False, False, False, True)

        OLD = 3
        SLOTS = E

        def expert_up_at(slot, new, old):
            if slot < OLD:
                return (2, E - OLD + slot) if old else None
            return (1, slot - OLD) if new else None

        def expert_down_at(slot, new, old):
            if slot <= OLD:
                return (2, E - OLD - 1 + slot) if old else None
            return (1, slot - OLD - 1) if new else None

        block = stack.enter_context(nc.Block())

        @block.sync
        def _(sp):
            def load_prepare(b):
                wait(sp, xn_made, b)
                sp.dma_start(x_ln[:], x[b].rearrange("(t p) d -> p t d", p=P)).then_inc(x_ln_in, 16)
                wait(sp, v_done, b)
                sp.dma_start(ctxT_in[:], ctx_t[b]).then_inc(ctx_in, 16)

            def load_residual(b):
                wait(sp, x1_made, b)
                sp.dma_start(x_res[:], x[b].rearrange("(t p) d -> p t d", p=P)).then_inc(x_res_in, 16)

            def to_stack(scratch, rows_of, landed):
                for odd in range(2):
                    for copy in range(2):
                        src = scratch(copy).rearrange("(j o d) c s -> o (d c) j s", o=2, d=DH)[odd]
                        sp.dma_start(rows_of(64 * odd + 32 * copy, odd).bitcast(F32), src).then_inc(landed, 16)

            def restack_k(b):
                sp.wait_ge(k_hi_made, b + 1)
                sp.wait_ge(k_lo_made, b + 1)
                for part, spilled in enumerate((k_spilled, k_spilled2)):
                    src = k_parts[:, part, :].bitcast(F32).unsqueeze(1).to_broadcast([P, 2, S])
                    sp.dma_start(k_scratch[part], src).then_inc(spilled, 16)
                sp.wait_ge(k_spilled, 16 * (b + 1))
                sp.wait_ge(k_spilled2, 16 * (b + 1))
                sp.wait_ge(stacks_free, 16 * (b + 1))
                to_stack(lambda copy: k_scratch[copy], lambda row, odd: k_stack[row:row + 32, :, :], k_stack_in)

            def restack_q(b):
                sp.wait_ge(q_hi_made, b + 1)
                sp.wait_ge(q_lo_made, b + 1)
                sp.dma_start(q_scratch, q_parts[:].bitcast(F32)).then_inc(q_spilled, 16)
                sp.wait_ge(q_spilled, 16 * (b + 1))
                to_stack(lambda copy: q_scratch, lambda row, odd: q_stack[row:row + 32, :, odd, :], q_stack_in)

            def store(b):
                sp.wait_ge(gated, E * (b + 1))
                sp.dma_start(out[b].rearrange("(t p) d -> p t d", p=P), y_out[:]).then_inc(stored, 16)

            def step(i, attend, prepare, new, old):
                if prepare:
                    load_prepare(i + 1)
                if attend:
                    load_residual(i)
                if prepare:
                    restack_k(i + 1)
                if old:
                    store(i - 2)
                if prepare:
                    restack_q(i + 1)

            sp.dma_start(x_ln[:], x[0].rearrange("(t p) d -> p t d", p=P)).then_inc(x_ln_in, 16)
            sp.dma_start(w_qkvo[:], w_attn).then_inc(wq_in, 16)
            sp.dma_start(ctxT_in[:], ctx_t[0]).then_inc(ctx_in, 16)
            sp.dma_start(wr_sb[:], wr).then_inc(small_in, 16)
            sp.dma_start(br_sb[:], br.unsqueeze(0).to_broadcast([P, E])).then_inc(small_in, 16)
            sp.dma_start(b1_sb[:], b1_t).then_inc(small_in, 16)
            sp.dma_start(b2_sb[:], b2).then_inc(small_in, 16)
            sp.dma_start(w1_sb[:], w1.rearrange("e d h -> d e h")).then_inc(w1_in, 16)
            sp.dma_start(w2_sb[:], w2.rearrange("e (c p) d -> p (e c) d", p=P)).then_inc(w2_in, 16)
            restack_k(0)
            restack_q(0)
            pipeline(sp, step)
            sp.wait_ge(stored, 16 * (B + 1))

        @block.tensor
        def _(pe):
            def transpose_xn(b, new):
                pe.wait_ge(xn_made, b + 1)
                if new:
                    pe.wait_ge(logits_made, b - 1)
                else:
                    pe.wait_ge(k_hi_made, b + 1)
                    pe.wait_ge(k_lo_made, b + 1)
                for t in range(TT):
                    mm = nc.tensor.transpose(misc_ps[:, t * P:(t + 1) * P], xn[:, t, :], ident[:])
                mm.then_inc(xnT_done, 1)

            def project_q(b):
                pe.wait_ge(xnT_taken, b + 1)
                nc.tensor.matmul(misc_ps[:, 0:S], w_qkvo[:, 0, :], xnT[:], start=True, stop=True).then_inc(q_done, 1)

            def project_k(b, new):
                pe.wait_ge(ctx_in, 16 * (b + 1))
                if new:
                    pe.wait_ge(x1_made, b - 1)
                elif b > 0:
                    pe.wait_ge(v_taken, b)
                nc.tensor.matmul(misc_ps[:, 0:S], w_qkvo[:, 1, :], ctxT_in[:], start=True, stop=True).then_inc(k_done, 1)

            def project_v(b):
                for t in range(TT):
                    mm = nc.tensor.matmul(misc_ps[:, S + t * P:S + (t + 1) * P], ctxT_in[:, t * P:(t + 1) * P],
                                          w_qkvo[:, 2, :], start=True, stop=True)
                mm.then_inc(v_done, 1)

            def scores(b, u):
                n, kt, qt = UNITS * b + u, u // TT, u % TT
                if u == 0:
                    pe.wait_ge(k_stack_in, 64 * (b + 1))
                    pe.wait_ge(q_stack_in, 64 * (b + 1))
                wait(pe, exp_made, n - 1)
                for j in range(PAIRS):
                    mm = nc.tensor.matmul(
                        score_ps[:, u % 2, 2 * j * P:(2 * j + 2) * P], k_stack[:, j, kt * P:(kt + 1) * P],
                        q_stack[:, j, :, qt * P:(qt + 1) * P], start=(j % 2 == 0), stop=True,
                        skip_group_check=True)
                mm.then_inc(scores_done, 1)

            def subtract_max(b, u):
                pe.wait_ge(max_made, UNITS * b + u + 1)
                m4 = shift_m[:, u % 2, :].unsqueeze(1).to_broadcast([P, BANK // P, P])
                for half in range(2):
                    mm = nc.tensor.matmul(score_ps[:, u % 2, half * BANK:(half + 1) * BANK], neg_ident[:], m4,
                                          start=False, stop=True, skip_group_check=True)
                    if u == UNITS - 2 and half == 0:
                        mm.then_inc(stacks_free, 16)
                mm.then_inc(shifted, 1)

            def attend_values(b, prepare, new):
                if new:
                    pe.wait_ge(b2_added, b)
                else:
                    pe.wait_ge(q_hi_made, b + 2)
                    pe.wait_ge(q_lo_made, b + 2)
                if prepare:
                    project_v(b + 1)
                pe.wait_ge(attn_made, UNITS * (b + 1))
                pe.wait_ge(v_taken, b + 1)
                for odd in range(2):
                    for kt in range(TT):
                        for g in range(PAIRS):
                            h = 2 * g + odd
                            mm = nc.tensor.matmul(misc_ps[32 * g:32 * g + 32, 0:S], v_pad[:, kt, h, :],
                                                  attn[:, kt, h, :], start=(odd == 0 and kt == 0),
                                                  stop=(odd == 1 and kt == TT - 1))
                mm.then_inc(av_done, 1)

            def project_out(b, attend):
                pe.wait_ge(heads_taken, b + 1)
                if attend:
                    pe.wait_ge(v_taken, b + 2)
                for t in range(TT):
                    mm = nc.tensor.matmul(misc_ps[:, t * P:(t + 1) * P], headsT[:, t * P:(t + 1) * P],
                                          w_qkvo[:, 3, :], start=True, stop=True)
                mm.then_inc(wo_done, 1)

            def transpose_x1n(b, prepare):
                pe.wait_ge(x1n_made, b + 1)
                if prepare:
                    pe.wait_ge(k_hi_made, b + 3)
                    pe.wait_ge(k_lo_made, b + 3)
                for t in range(TT):
                    mm = nc.tensor.transpose(misc_ps[:, t * P:(t + 1) * P], x1n[:, t, :], ident[:])
                mm.then_inc(x1T_done, 1)

            def route(b):
                pe.wait_ge(x1T_hi_made, b + 1)
                pe.wait_ge(x1T_lo_made, b + 1)
                if isinstance(b, int) and b == 0:
                    pe.wait_ge(wr_hi_made, 1)
                    pe.wait_ge(wr_lo_made, 1)
                for t in range(TT):
                    for n, (xt, w) in enumerate(((x1T_lo, wr_lo), (x1T_lo, wr_hi), (x1T_hi, wr_lo), (x1T_hi, wr_hi))):
                        mm = nc.tensor.matmul(misc_ps[:, t * E:(t + 1) * E], xt[:, t * P:(t + 1) * P], w[:],
                                              start=(n == 0), stop=(n == 3))
                mm.then_inc(router_done, 1)

            def transpose_gates(b, prepare):
                pe.wait_ge(gates_made, b + 1)
                if prepare:
                    pe.wait_ge(xnT_taken, b + 3)
                for t in range(TT):
                    mm = nc.tensor.transpose(misc_ps[0:E, S + t * P:S + (t + 1) * P], gates[:, t, :], ident[:])
                mm.then_inc(gatesT_done, 1)

            def gated_b2(b, prepare):
                pe.wait_ge(gatesT_taken, b + 1)
                if prepare:
                    pe.wait_ge(q_hi_made, b + 3)
                    pe.wait_ge(q_lo_made, b + 3)
                for t in range(TT):
                    mm = nc.tensor.matmul(misc_ps[:, t * P:(t + 1) * P], gatesT[:, t * P:(t + 1) * P], b2_sb[:],
                                          start=True, stop=True)
                mm.then_inc(b2_done, 1)

            def expert_up(b, e):
                n = E * b + e
                if e == 0:
                    pe.wait_ge(x1T_hi_made, b + 1)
                    pe.wait_ge(x1T_lo_made, b + 1)
                if e == 0 and isinstance(b, int) and b == 0:
                    pe.wait_ge(w1_hi_made, 1)
                    pe.wait_ge(w1_lo_made, 1)
                wait(pe, relu_made, n)
                for c in range(HC):
                    for k, (w, xt) in enumerate(((w1_lo, x1T_hi), (w1_hi, x1T_lo), (w1_hi, x1T_hi))):
                        mm = nc.tensor.matmul(h_ps[:, c * S:(c + 1) * S], w[:, e, c * P:(c + 1) * P], xt[:],
                                              start=(k == 0), stop=(k == 2))
                mm.then_inc(h_done, 1)

            def expert_down(b, e):
                n = E * b + e
                pe.wait_ge(relu_made, n + 1)
                wait(pe, gated, n - 1)
                for t in range(TT):
                    for c in range(HC):
                        mm = nc.tensor.matmul(y_ps[:, e % 2, t * D:(t + 1) * D], hT[:, e % 2, c, t * P:(t + 1) * P],
                                              w2_sb[:, e * HC + c, :], start=(c == 0), stop=(c == HC - 1))
                mm.then_inc(y_done, 1)

            def step(i, attend, prepare, new, old):
                for slot in range(SLOTS):
                    if up := expert_up_at(slot, new, old):
                        expert_up(i - up[0], up[1])
                    if down := expert_down_at(slot, new, old):
                        expert_down(i - down[0], down[1])
                    if slot == 0:
                        if attend:
                            scores(i, 0)
                            scores(i, 1)
                        if new:
                            project_out(i - 1, attend)
                    if slot == 1:
                        if attend:
                            subtract_max(i, 0)
                        if prepare:
                            project_k(i + 1, new)
                        if attend:
                            subtract_max(i, 1)
                    if slot == 2:
                        if new:
                            transpose_x1n(i - 1, prepare)
                        if attend:
                            scores(i, 2)
                            scores(i, 3)
                    if slot == 3:
                        if new:
                            route(i - 1)
                        if attend:
                            subtract_max(i, 2)
                    if slot == 4:
                        if attend:
                            subtract_max(i, 3)
                        if prepare:
                            transpose_xn(i + 1, new)
                    if slot == 5:
                        if new:
                            transpose_gates(i - 1, prepare)
                        if prepare:
                            project_q(i + 1)
                    if slot == 6 and new:
                        gated_b2(i - 1, prepare)
                    if slot == 7 and attend:
                        attend_values(i, prepare, new)

            pe.wait_ge(ident_made, 1)
            pe.wait_ge(wq_in, 16)
            project_k(0, False)
            transpose_xn(0, False)
            project_q(0)
            pe.wait_ge(q_hi_made, 1)
            pe.wait_ge(q_lo_made, 1)
            project_v(0)
            pe.wait_ge(neg_ident_made, 1)
            pe.wait_ge(w2_in, 16)
            pe.wait_ge(small_in, 64)
            pipeline(pe, step)

        @block.scalar
        def _(act):
            def take(dst, src, done, b, made):
                act.wait_ge(done, b + 1)
                nc.scalar.activation(dst, src, ACT.Copy).then_inc(made, 1)

            def take_xnT(b):
                wait(act, q_done, b)
                take(xnT[:], misc_ps[:, 0:S], xnT_done, b, xnT_taken)

            def take_q_hi(b):
                wait(act, q_spilled, 16 * b)
                take(q_parts[:, 0, :], misc_ps[:, 0:S], q_done, b, q_hi_made)

            def take_k_hi(b):
                wait(act, k_spilled, 16 * b)
                take(k_parts[:, 0, :], misc_ps[:, 0:S], k_done, b, k_hi_made)

            def take_v(b):
                wait(act, av_done, b)
                if isinstance(b, int) and b == 0:
                    act.wait_ge(v_zeroed, 1)
                dst = v_pad[:].rearrange("p k (j o) (a d) -> p (k j) (o a) d", o=2, d=DH)[:, :, 0:4:3, :]
                take(dst, misc_ps[:, S:2 * S].rearrange("p (n o d) -> p n o d", o=2, d=DH), v_done, b, v_taken)

            def exponentiate(b, u):
                n = UNITS * b + u
                act.wait_ge(shifted, n + 1)
                wait(act, attn_made, n - UNITS + 1)
                nc.scalar.activation(e_sb[:, u, :], score_ps[:, u % 2, :], ACT.Exp, scale=SCALE).then_inc(exp_made, 1)

            def invert_sum(b, u):
                n = UNITS * b + u
                act.wait_ge(sum_made, n + 1)
                nc.scalar.activation(log_sum[:, u, :], e_sum[:, u, :], ACT.Ln).then_inc(log_made, 1)
                act.wait_ge(log_made, n + 1)
                nc.scalar.activation(e_rcp[:, u, :], log_sum[:, u, :], ACT.Exp, scale=-1.0).then_inc(rcp_made, 1)

            def take_heads(b):
                wait(act, wo_done, b)
                take(headsT[:], misc_ps[:, 0:S], av_done, b, heads_taken)

            def take_x1T_hi(b):
                wait(act, h_done, E * b)
                take(x1T_hi[:], misc_ps[:, 0:S], x1T_done, b, x1T_hi_made)

            def router_exp(b):
                act.wait_ge(rel_made, b + 1)
                nc.scalar.activation(rel_exp[:], rel[:], ACT.Exp).then_inc(rel_exp_made, 1)

            def take_gatesT(b, prepare):
                wait(act, b2_done, b)
                if prepare:
                    act.wait_ge(q_done, b + 3)
                take(gatesT[:], misc_ps[0:E, S:2 * S], gatesT_done, b, gatesT_taken)

            def relu(b, e):
                n = E * b + e
                act.wait_ge(h_done, n + 1)
                wait(act, y_done, n - 1)
                for c in range(HC):
                    op = nc.scalar.activation(hT[:, e % 2, c, :], h_ps[:, c * S:(c + 1) * S], ACT.Relu,
                                              bias=b1_sb[:, e * HC + c:e * HC + c + 1])
                op.then_inc(relu_made, 1)

            def step(i, attend, prepare, new, old):
                for slot in range(SLOTS):
                    if up := expert_up_at(slot, new, old):
                        relu(i - up[0], up[1])
                    if slot == 1:
                        if attend:
                            exponentiate(i, 0)
                        if prepare:
                            take_k_hi(i + 1)
                    if slot == 2:
                        if attend:
                            exponentiate(i, 1)
                        if new:
                            take_x1T_hi(i - 1)
                    if slot == 3 and attend:
                        invert_sum(i, 0)
                        exponentiate(i, 2)
                    if slot == 4:
                        if attend:
                            invert_sum(i, 1)
                        if new:
                            router_exp(i - 1)
                        if attend:
                            exponentiate(i, 3)
                        if prepare:
                            take_xnT(i + 1)
                    if slot == 5:
                        if new:
                            take_gatesT(i - 1, prepare)
                        if prepare:
                            take_q_hi(i + 1)
                        if attend:
                            invert_sum(i, 2)
                    if slot == 6 and attend:
                        invert_sum(i, 3)
                    if slot == 7:
                        if attend:
                            take_heads(i)
                        if prepare:
                            take_v(i + 1)

            nc.scalar.preload_act_table_set("natural_log_exp_and_others")
            act.wait_ge(small_in, 64)
            take_k_hi(0)
            take_xnT(0)
            take_q_hi(0)
            take_v(0)
            pipeline(act, step)

        @block.vector
        def _(dve):
            def norm_stats(src, stats, step_sem):
                for t in range(TT):
                    op = nc.vector.bn_stats(stats[:, t, :], src[:, t, :])
                op.then_inc(step_sem, 1)

            def norm_var(b, stats, mv, var, step_sem, var_made):
                for t in range(TT):
                    op = nc.vector.bn_aggr(mv[:, t, :], stats[:, t, :])
                op.then_inc(step_sem, 1)
                dve.wait_ge(step_sem, 2 * b + 2)
                nc.vector.tensor_scalar(var[:], mv[:, :, 1], EPS, None, ALU.add).then_inc(var_made, 1)

            def norm_apply(src, mv, rstd, dst, made):
                for t in range(TT):
                    op = nc.vector.tensor_scalar(dst[:, t, :], src[:, t, :], mv[:, t, 0:1], rstd[:, t:t + 1],
                                                 ALU.subtract, ALU.mult)
                op.then_inc(made, 1)

            def ln1_begin(b):
                dve.wait_ge(x_ln_in, 16 * (b + 1))
                norm_stats(x_ln, ln1_stats, ln1_step)

            def ln1_end(b):
                dve.wait_ge(ln1_rstd_made, b + 1)
                wait(dve, xnT_done, b)
                norm_apply(x_ln, ln1_mv, ln1_rstd, xn, xn_made)

            def ln2_begin(b):
                dve.wait_ge(wo_done, b + 1)
                dve.wait_ge(x_res_in, 16 * (b + 1))
                wait(dve, gated, E * b - E + 1)
                nc.vector.tensor_tensor(x1[:].rearrange("p t d -> p (t d)"), misc_ps[:, 0:S],
                                        x_res[:].rearrange("p t d -> p (t d)"), ALU.add).then_inc(x1_made, 1)
                dve.wait_ge(x1_made, b + 1)
                norm_stats(x1, ln2_stats, ln2_step)

            def ln2_end(b):
                dve.wait_ge(ln2_rstd_made, b + 1)
                wait(dve, x1T_done, b)
                norm_apply(x1, ln2_mv, ln2_rstd, x1n, x1n_made)

            def low_part(dst, hi, hi_made, b, made):
                dve.wait_ge(hi_made, b + 1)
                nc.vector.tensor_tensor(dst, misc_ps[:, 0:S], hi.bitcast(F32), ALU.subtract).then_inc(made, 1)

            def q_lo(b):
                low_part(q_parts[:, 1, :], q_parts[:, 0, :], q_hi_made, b, q_lo_made)

            def k_lo(b):
                low_part(k_parts[:, 1, :], k_parts[:, 0, :], k_hi_made, b, k_lo_made)

            def x1T_low(b):
                wait(dve, h_done, E * b)
                low_part(x1T_lo[:], x1T_hi[:], x1T_hi_made, b, x1T_lo_made)

            def head_max(b, u):
                dve.wait_ge(scores_done, UNITS * b + u + 1)
                nc.vector.tensor_reduce(shift_m[:, u % 2, :], score_ps[:, u % 2, :].rearrange("p (h q) -> p q h", h=H),
                                        AX.X, ALU.max).then_inc(max_made, 1)

            def normalize(b, u):
                kt, qt = u // TT, u % TT
                dve.wait_ge(rcp_made, UNITS * b + u + 1)
                if u == 0:
                    wait(dve, av_done, b)
                nc.vector.tensor_tensor(attn[:, kt, :, qt * P:(qt + 1) * P],
                                        e_sb[:, u, :].rearrange("p (h q) -> p h q", h=H),
                                        e_rcp[:, u, :].unsqueeze(1).to_broadcast([P, H, P]),
                                        ALU.mult).then_inc(attn_made, 1)

            def take_logits(b):
                dve.wait_ge(router_done, b + 1)
                nc.vector.tensor_tensor(logits[:], misc_ps[:, 0:TT * E].rearrange("p (t e) -> p t e", e=E),
                                        br_sb[:].unsqueeze(1).to_broadcast([P, TT, E]), ALU.add).then_inc(logits_made, 1)

            def choose_experts(b):
                at = ROUTER_STEPS * b
                for t in range(TT):
                    op = nc.vector.max(top8[:, t, :], logits[:, t, :])
                op.then_inc(router_step, 1)
                dve.wait_ge(router_step, at + 1)
                nc.vector.tensor_tensor(rel[:], logits[:], top8[:, :, 0:1].to_broadcast([P, TT, E]),
                                        ALU.subtract).then_inc(rel_made, 1)
                for t in range(TT):
                    op = nc.vector.max_index(top8_at[:, t, :], top8[:, t, :], logits[:, t, :])
                op.then_inc(router_step, 1)
                dve.wait_ge(router_step, at + 2)
                nc.vector.tensor_copy(top8_at_f[:], top8_at[:]).then_inc(router_step, 1)
                dve.wait_ge(router_step, at + 3)
                for n, place in enumerate((first, second)):
                    nc.vector.tensor_tensor(place[:], iota8[:].unsqueeze(1).to_broadcast([P, TT, E]),
                                            top8_at_f[:, :, n:n + 1].to_broadcast([P, TT, E]),
                                            ALU.is_equal).then_inc(router_step, 1)
                dve.wait_ge(router_step, at + 5)
                nc.vector.tensor_tensor(chosen[:], first[:], second[:], ALU.add).then_inc(router_step, 1)

            def make_gates(b):
                at = ROUTER_STEPS * b
                dve.wait_ge(rel_exp_made, b + 1)
                dve.wait_ge(router_step, at + 6)
                nc.vector.tensor_tensor(chosen_exp[:], rel_exp[:], chosen[:], ALU.mult).then_inc(router_step, 1)
                dve.wait_ge(router_step, at + 7)
                nc.vector.tensor_reduce(gate_sum[:], chosen_exp[:], AX.X, ALU.add).then_inc(router_step, 1)
                dve.wait_ge(router_step, at + 8)
                nc.vector.reciprocal(gate_rcp[:], gate_sum[:]).then_inc(router_step, 1)
                dve.wait_ge(router_step, at + 9)
                nc.vector.tensor_tensor(gates[:], chosen_exp[:], gate_rcp[:].unsqueeze(2).to_broadcast([P, TT, E]),
                                        ALU.mult).then_inc(gates_made, 1)

            def add_expert(b, e):
                n = E * b + e
                dve.wait_ge(y_done, n + 1)
                wait(dve, gated, n)
                if e == 0:
                    dve.wait_ge(gates_made, b + 1)
                if e == B2_AFTER + 1:
                    dve.wait_ge(b2_added, b + 1)
                if e == E - 1:
                    dve.wait_ge(stored, 16 * (b + 1))
                src = x1 if e == 0 else acc
                dst = y_out if e == E - 1 else acc
                for t in range(TT):
                    op = nc.vector.scalar_tensor_tensor(out=dst[:, t, :], in0=y_ps[:, e % 2, t * D:(t + 1) * D],
                                                        scalar=gates[:, t, e:e + 1], in1=src[:, t, :],
                                                        op0=ALU.mult, op1=ALU.add)
                op.then_inc(gated, 1)

            def add_b2(b):
                dve.wait_ge(b2_done, b + 1)
                dve.wait_ge(gated, E * b + B2_AFTER + 1)
                nc.vector.tensor_tensor(acc[:].rearrange("p t d -> p (t d)"), misc_ps[:, 0:S],
                                        acc[:].rearrange("p t d -> p (t d)"), ALU.add).then_inc(b2_added, 1)

            def step(i, attend, prepare, new, old):
                f, g = i - 1, i - 2
                if attend:
                    head_max(i, 0)
                if new:
                    ln2_begin(f)
                    dve.wait_ge(ln2_step, 2 * f + 1)
                if attend:
                    head_max(i, 1)
                if new:
                    norm_var(f, ln2_stats, ln2_mv, ln2_var, ln2_step, ln2_var_made)
                if old:
                    add_expert(g, 4)
                if prepare:
                    k_lo(i + 1)
                if old:
                    add_expert(g, 5)
                if new:
                    ln2_end(f)
                if attend:
                    head_max(i, 2)
                if new:
                    x1T_low(f)
                if old:
                    add_expert(g, 6)
                if attend:
                    head_max(i, 3)
                    normalize(i, 0)
                if prepare:
                    ln1_begin(i + 1)
                    dve.wait_ge(ln1_step, 2 * i + 3)
                if new:
                    take_logits(f)
                    dve.wait_ge(logits_made, f + 1)
                if old:
                    add_expert(g, 7)
                if prepare:
                    norm_var(i + 1, ln1_stats, ln1_mv, ln1_var, ln1_step, ln1_var_made)
                if new:
                    choose_experts(f)
                if attend:
                    normalize(i, 1)
                if new:
                    make_gates(f)
                if prepare:
                    ln1_end(i + 1)
                if new:
                    add_expert(f, 0)
                if prepare:
                    q_lo(i + 1)
                if attend:
                    normalize(i, 2)
                if new:
                    add_expert(f, 1)
                    add_expert(f, 2)
                    add_b2(f)
                if attend:
                    normalize(i, 3)
                if new:
                    add_expert(f, 3)

            ln1_begin(0)
            dve.wait_ge(ln1_step, 1)
            norm_var(0, ln1_stats, ln1_mv, ln1_var, ln1_step, ln1_var_made)
            nc.vector.memset(q_stack[:].bitcast(F32), 0.0).then_inc(stacks_free, 16)
            nc.vector.memset(v_pad[:], 0.0).then_inc(v_zeroed, 1)
            nc.vector.memset(y_out[:], 0.0).then_inc(stored, 16)
            ln1_end(0)
            dve.wait_ge(ident_made, 1)
            nc.vector.tensor_scalar(neg_ident[:], ident[:], -1.0, None, ALU.mult).then_inc(neg_ident_made, 1)
            k_lo(0)
            q_lo(0)
            dve.wait_ge(small_in, 64)
            nc.vector.tensor_copy(wr_hi[:], wr_sb[:]).then_inc(wr_hi_made, 1)
            dve.wait_ge(wr_hi_made, 1)
            nc.vector.tensor_tensor(wr_lo[:], wr_sb[:], wr_hi[:].bitcast(F32), ALU.subtract).then_inc(wr_lo_made, 1)
            dve.wait_ge(w1_in, 16)
            nc.vector.tensor_copy(w1_hi[:], w1_sb[:]).then_inc(w1_hi_made, 1)
            dve.wait_ge(pool_made, 1)
            pipeline(dve, step)

        @block.gpsimd
        def _(pool):
            def rstd(b, var, var_made, dst, made):
                pool.wait_ge(var_made, b + 1)
                nc.gpsimd.tensor_tensor(dst[:], var[:], neg_half[:], ALU.pow).then_inc(made, 1)

            def head_sum(b, u):
                n = UNITS * b + u
                pool.wait_ge(exp_made, n + 1)
                e = e_sb[:, u, :]
                nc.gpsimd.tensor_tensor(half_sum[:], e[:, 0:HQ // 2], e[:, HQ // 2:HQ], ALU.add).then_inc(sum_step, 1)
                pool.wait_ge(sum_step, 2 * n + 1)
                nc.gpsimd.tensor_tensor(quarter_sum[:], half_sum[:, 0:HQ // 4], half_sum[:, HQ // 4:HQ // 2],
                                        ALU.add).then_inc(sum_step, 1)
                pool.wait_ge(sum_step, 2 * n + 2)
                nc.gpsimd.tensor_tensor(e_sum[:, u, :], quarter_sum[:, 0:P], quarter_sum[:, P:2 * P],
                                        ALU.add).then_inc(sum_made, 1)

            def step(i, attend, prepare, new, old):
                if new:
                    rstd(i - 1, ln2_var, ln2_var_made, ln2_rstd, ln2_rstd_made)
                if attend:
                    head_sum(i, 0)
                    head_sum(i, 1)
                if prepare:
                    rstd(i + 1, ln1_var, ln1_var_made, ln1_rstd, ln1_rstd_made)
                if attend:
                    head_sum(i, 2)
                    head_sum(i, 3)

            nc.gpsimd.memset(neg_half[:], -0.5).then_inc(zeroed, 1)
            nc.gpsimd.memset(ident[:], 0.0).then_inc(zeroed, 1)
            pool.wait_ge(zeroed, 2)
            nc.gpsimd.affine_select(out=ident[:], in_=ident[:], compare_op=ALU.not_equal, fill=1.0, base=0,
                                    pattern=[[-1, P]], channel_multiplier=1).then_inc(ident_made, 1)
            rstd(0, ln1_var, ln1_var_made, ln1_rstd, ln1_rstd_made)
            for e in range(E):
                op = nc.gpsimd.memset(iota8[:, e:e + 1], float(e))
            op.then_inc(pool_made, 1)
            pool.wait_ge(w1_hi_made, 1)
            nc.gpsimd.tensor_tensor(w1_lo[:], w1_sb[:], w1_hi[:].bitcast(F32), ALU.subtract).then_inc(w1_lo_made, 1)
            pipeline(pool, step)


def kernel(x, ctx_1024, L0_xattn_W_Q, L0_xattn_W_K, L0_xattn_W_V, L0_xattn_W_O, L0_ffn_Wr, L0_ffn_br,
           L0_ffn_W1, L0_ffn_b1, L0_ffn_W2, L0_ffn_b2):
    import numpy as np
    import concourse.bacc as bacc
    from concourse.bass_utils import run_bass_kernel_spmd

    E, HID = L0_ffn_b1.shape
    w_attn = np.stack([np.asarray(w).T for w in (L0_xattn_W_Q, L0_xattn_W_K, L0_xattn_W_V, L0_xattn_W_O)], axis=1)
    given = {
        "x": x,
        "ctx_t": np.asarray(ctx_1024).transpose(0, 2, 1),
        "w_attn": w_attn,
        "wr": L0_ffn_Wr,
        "br": L0_ffn_br,
        "w1": L0_ffn_W1,
        "b1_t": np.asarray(L0_ffn_b1).reshape(E * HID // P, P).T,
        "w2": L0_ffn_W2,
        "b2": L0_ffn_b2,
    }
    nc = bacc.Bacc("TRN2", target_bir_lowering=False, num_devices=1)
    arrays, args = {}, []
    for name, a in given.items():
        a = np.ascontiguousarray(a)
        arrays[f"in_{name}"] = a
        args.append(nc.dram_tensor(f"in_{name}", a.shape, mybir.dt.from_np(a.dtype), kind="ExternalInput").ap())
    shape = tuple(np.asarray(x).shape)
    args.append(nc.dram_tensor("out_y", shape, F32, kind="ExternalOutput").ap())
    build(nc, *args)
    r = run_bass_kernel_spmd(nc, [arrays], core_ids=[0])
    return r.results[0]["out_y"]
```

```python
from contextlib import ExitStack

import concourse.bass as bass
from concourse import mybir

F32 = mybir.dt.float32
F32R = mybir.dt.float32r
U32 = mybir.dt.uint32
ALU = mybir.AluOpType
ACT = mybir.ActivationFunctionType
AX = mybir.AxisListType

P = 128
EPS = 1e-5


def build(nc, x, ctx_t, w_attn, wr, br, w1, b1_t, w2, b2, out):
    B, S, D = x.shape
    H, DH = 8, D // 8
    E, HID = w1.shape[0], w1.shape[2]
    TT = S // P
    HC = HID // P
    PAIRS = H // 2
    UNITS = TT * TT
    HQ = H * P
    BANK = 512
    SCALE = float(DH) ** -0.5
    assert D == P and S == 256 and UNITS == 4

    with ExitStack() as stack:
        def sb(name, shape, dt=F32):
            return stack.enter_context(nc.sbuf_tensor(name, shape, dt))

        def ps(name, shape, dt=F32):
            return stack.enter_context(nc.psum_tensor(name, shape, dt))

        def sem(name):
            return stack.enter_context(nc.semaphore(name))

        ident = sb("ident", [P, P])
        neg_ident = sb("neg_ident", [P, P], F32R)
        iota8 = sb("iota8", [P, E])
        neg_half = sb("neg_half", [P, TT])
        w_qkvo = sb("w_qkvo", [P, 4, D])
        w1_sb = sb("w1_sb", [P, E, HID])
        w1_hi = sb("w1_hi", [P, E, HID], F32R)
        w1_lo = sb("w1_lo", [P, E, HID], F32R)
        b1_sb = sb("b1_sb", [P, E * HC])
        w2_sb = sb("w2_sb", [P, E * HC, D])
        b2_sb = sb("b2_sb", [E, D])
        wr_sb = sb("wr_sb", [P, E])
        wr_hi = sb("wr_hi", [P, E], F32R)
        wr_lo = sb("wr_lo", [P, E], F32R)
        br_sb = sb("br_sb", [P, E])

        x_ln = sb("x_ln", [P, TT, D])
        ctxT_in = sb("ctxT_in", [P, S])
        ln1_stats = sb("ln1_stats", [P, TT, 6])
        ln1_mv = sb("ln1_mv", [P, TT, 2])
        ln1_var = sb("ln1_var", [P, TT])
        ln1_rstd = sb("ln1_rstd", [P, TT])
        x_centred = sb("x_centred", [P, TT, D])
        xn = sb("xn", [P, TT, D])
        xnT = sb("xnT", [P, S])
        q_parts = sb("q_parts", [P, 2, S], F32R)
        k_parts = sb("k_parts", [P, 2, S], F32R)
        k_stack = sb("k_stack", [P, PAIRS, S], F32R)
        q_stack = sb("q_stack", [P, PAIRS, 2, S], F32R)
        v_pad = sb("v_pad", [P, TT, H, 32])
        q_scratch = nc.dram_tensor("q_scratch", (P, 2, S), F32, kind="Internal").ap()
        k_scratch = nc.dram_tensor("k_scratch", (2, P, 2, S), F32, kind="Internal").ap()

        shift_m = sb("shift_m", [P, 2, P], F32R)
        e_sb = sb("e_sb", [P, UNITS, HQ])
        half_sum = sb("half_sum", [P, HQ // 2])
        quarter_sum = sb("quarter_sum", [P, HQ // 4])
        e_sum = sb("e_sum", [P, UNITS, P])
        log_sum = sb("log_sum", [P, UNITS, P])
        e_rcp = sb("e_rcp", [P, UNITS, P])
        attn = sb("attn", [P, TT, H, S])
        headsT = sb("headsT", [P, S])
        x_res = sb("x_res", [P, TT, D])
        x1 = sb("x1", [P, TT, D])

        ln2_stats = sb("ln2_stats", [P, TT, 6])
        ln2_mv = sb("ln2_mv", [P, TT, 2])
        ln2_var = sb("ln2_var", [P, TT])
        ln2_rstd = sb("ln2_rstd", [P, TT])
        x1n = sb("x1n", [P, TT, D])
        x1T_hi = sb("x1T_hi", [P, S], F32R)
        x1T_lo = sb("x1T_lo", [P, S], F32R)
        logits = sb("logits", [P, TT, E])
        top8 = sb("top8", [P, TT, 8])
        top8_at = sb("top8_at", [P, TT, 8], U32)
        top8_at_f = sb("top8_at_f", [P, TT, 8])
        rel = sb("rel", [P, TT, E])
        first = sb("first", [P, TT, E])
        second = sb("second", [P, TT, E])
        chosen = sb("chosen", [P, TT, E])
        rel_exp = sb("rel_exp", [P, TT, E])
        chosen_exp = sb("chosen_exp", [P, TT, E])
        gate_sum = sb("gate_sum", [P, TT])
        gate_rcp = sb("gate_rcp", [P, TT])
        gates = sb("gates", [P, TT, E])
        gatesT = sb("gatesT", [E, S])
        hT = sb("hT", [P, 2, HC, S])
        acc = sb("acc", [P, TT, D])
        y_out = sb("y_out", [P, TT, D])

        score_ps = ps("score_ps", [P, 2, HQ])
        h_ps = ps("h_ps", [P, HC * S])
        y_ps = ps("y_ps", [P, 2, BANK])
        misc_ps = ps("misc_ps", [P, BANK])

        wq_in, w1_in, w2_in, small_in = sem("wq_in"), sem("w1_in"), sem("w2_in"), sem("small_in")
        x_ln_in, x_res_in, ctx_in = sem("x_ln_in"), sem("x_res_in"), sem("ctx_in")
        zeroed, ident_made, pool_made = sem("zeroed"), sem("ident_made"), sem("pool_made")
        neg_ident_made, v_zeroed, stacks_free = sem("neg_ident_made"), sem("v_zeroed"), sem("stacks_free")
        w1_hi_made, w1_lo_made, wr_hi_made, wr_lo_made = (
            sem("w1_hi_made"), sem("w1_lo_made"), sem("wr_hi_made"), sem("wr_lo_made"))
        ln1_step, ln1_var_made, ln1_rstd_made, xn_made = (
            sem("ln1_step"), sem("ln1_var_made"), sem("ln1_rstd_made"), sem("xn_made"))
        xnT_done, xnT_taken = sem("xnT_done"), sem("xnT_taken")
        q_done, q_hi_made, q_lo_made, q_spilled = (
            sem("q_done"), sem("q_hi_made"), sem("q_lo_made"), sem("q_spilled"))
        k_done, k_hi_made, k_lo_made, k_spilled = (
            sem("k_done"), sem("k_hi_made"), sem("k_lo_made"), sem("k_spilled"))
        k_spilled2, k_stack_in, q_stack_in = sem("k_spilled2"), sem("k_stack_in"), sem("q_stack_in")
        v_done, v_taken = sem("v_done"), sem("v_taken")
        scores_done, max_made, shifted, exp_made = (
            sem("scores_done"), sem("max_made"), sem("shifted"), sem("exp_made"))
        sum_step, sum_made, log_made, rcp_made, attn_made = (
            sem("sum_step"), sem("sum_made"), sem("log_made"), sem("rcp_made"), sem("attn_made"))
        attn0_made, centred = sem("attn0_made"), sem("centred")
        av_done, heads_taken, wo_done, x1_made = (
            sem("av_done"), sem("heads_taken"), sem("wo_done"), sem("x1_made"))
        ln2_step, ln2_var_made, ln2_rstd_made, x1n_made = (
            sem("ln2_step"), sem("ln2_var_made"), sem("ln2_rstd_made"), sem("x1n_made"))
        x1T_done, x1T_hi_made, x1T_lo_made = sem("x1T_done"), sem("x1T_hi_made"), sem("x1T_lo_made")
        router_done, logits_made, router_step, rel_made, rel_exp_made, gates_made = (
            sem("router_done"), sem("logits_made"), sem("router_step"), sem("rel_made"),
            sem("rel_exp_made"), sem("gates_made"))
        gatesT_done, gatesT_taken, b2_done, b2_added = (
            sem("gatesT_done"), sem("gatesT_taken"), sem("b2_done"), sem("b2_added"))
        h_done, relu_made, y_done, gated, stored = (
            sem("h_done"), sem("relu_made"), sem("y_done"), sem("gated"), sem("stored"))
        ROUTER_STEPS = 9
        SUMS_BY_DVE = UNITS - 1
        B2_AFTER = 1

        def wait(eng, semaphore, n):
            if not (isinstance(n, int) and n <= 0):
                eng.wait_ge(semaphore, n)

        def pipeline(eng, step):
            step(0, True, True, False, False)
            step(1, True, True, True, False)
            with eng.Fori(2, B - 1) as i:
                step(i, True, True, True, True)
            step(B - 1, True, False, True, True)
            step(B, False, False, True, True)
            step(B + 1, False, False, False, True)

        OLD = 3
        SLOTS = E

        def expert_up_at(slot, new, old):
            if slot < OLD:
                return (2, E - OLD + slot) if old else None
            return (1, slot - OLD) if new else None

        def expert_down_at(slot, new, old):
            if slot <= OLD:
                return (2, E - OLD - 1 + slot) if old else None
            return (1, slot - OLD - 1) if new else None

        block = stack.enter_context(nc.Block())

        @block.sync
        def _(sp):
            def load_tokens(b):
                wait(sp, xn_made, b)
                sp.dma_start(x_ln[:], x[b].rearrange("(t p) d -> p t d", p=P)).then_inc(x_ln_in, 16)

            def load_context(b):
                wait(sp, v_done, b)
                sp.dma_start(ctxT_in[:], ctx_t[b]).then_inc(ctx_in, 16)

            def load_residual(b):
                wait(sp, x1_made, b)
                sp.dma_start(x_res[:], x[b].rearrange("(t p) d -> p t d", p=P)).then_inc(x_res_in, 16)

            def spill_k(b):
                sp.wait_ge(k_hi_made, b + 1)
                sp.wait_ge(k_lo_made, b + 1)
                for part, spilled in enumerate((k_spilled, k_spilled2)):
                    src = k_parts[:, part, :].bitcast(F32).unsqueeze(1).to_broadcast([P, 2, S])
                    sp.dma_start(k_scratch[part], src).then_inc(spilled, 16)

            def load_k_stack(b):
                sp.wait_ge(k_spilled, 16 * (b + 1))
                sp.wait_ge(k_spilled2, 16 * (b + 1))
                sp.wait_ge(stacks_free, 16 * (b + 1))
                for copy in range(2):
                    src = k_scratch[copy].rearrange("(j r) c s -> (r c) j s", r=2 * DH)
                    sp.dma_start(k_stack[64 * copy:64 * copy + 64, :, :].bitcast(F32), src).then_inc(k_stack_in, 16)

            def spill_q(b):
                sp.wait_ge(q_hi_made, b + 1)
                sp.wait_ge(q_lo_made, b + 1)
                sp.dma_start(q_scratch, q_parts[:].bitcast(F32)).then_inc(q_spilled, 16)

            def load_q_stack(b):
                sp.wait_ge(q_spilled, 16 * (b + 1))
                src = q_scratch.rearrange("(j o d) c s -> o (d c) j s", o=2, d=DH)
                for copy in range(2):
                    for odd in range(2):
                        row = 64 * copy + 32 * odd
                        sp.dma_start(q_stack[row:row + 32, :, odd, :].bitcast(F32), src[odd]).then_inc(q_stack_in, 16)

            def store(b):
                sp.wait_ge(gated, E * (b + 1))
                sp.dma_start(out[b].rearrange("(t p) d -> p t d", p=P), y_out[:]).then_inc(stored, 16)

            def step(i, attend, prepare, new, old):
                if prepare and new:
                    load_tokens(i + 1)
                    load_context(i + 1)
                if attend:
                    load_residual(i)
                if prepare and not new:
                    sp.dma_start(w1_sb[:], w1.rearrange("e d h -> d e h")).then_inc(w1_in, 16)
                if prepare:
                    spill_k(i + 1)
                    load_k_stack(i + 1)
                    spill_q(i + 1)
                    load_q_stack(i + 1)
                if prepare and not new:
                    sp.dma_start(w2_sb[:], w2.rearrange("e (c p) d -> p (e c) d", p=P)).then_inc(w2_in, 16)
                if old:
                    store(i - 2)

            sp.dma_start(w_qkvo[:], w_attn).then_inc(wq_in, 16)
            load_tokens(0)
            sp.dma_start(ctxT_in[:], ctx_t[0]).then_inc(ctx_in, 16)
            sp.dma_start(wr_sb[:], wr).then_inc(small_in, 16)
            sp.dma_start(br_sb[:], br.unsqueeze(0).to_broadcast([P, E])).then_inc(small_in, 16)
            sp.dma_start(b1_sb[:], b1_t).then_inc(small_in, 16)
            sp.dma_start(b2_sb[:], b2).then_inc(small_in, 16)
            spill_k(0)
            load_tokens(1)
            spill_q(0)
            load_k_stack(0)
            load_context(1)
            load_q_stack(0)
            pipeline(sp, step)
            sp.wait_ge(stored, 16 * (B + 1))

        @block.tensor
        def _(pe):
            def transpose_tokens(b1, b2):
                if b1 is not None:
                    pe.wait_ge(xn_made, b1 + 1)
                    pe.wait_ge(k_hi_made, b1 + 1)
                    pe.wait_ge(k_lo_made, b1 + 1)
                if b2 is not None:
                    pe.wait_ge(x1n_made, b2 + 1)
                if b1 is not None:
                    for t in range(TT):
                        mm = nc.tensor.transpose(misc_ps[:, t * P:(t + 1) * P], xn[:, t, :], ident[:])
                    mm.then_inc(xnT_done, 1)
                if b2 is not None:
                    for t in range(TT):
                        mm = nc.tensor.transpose(misc_ps[:, S + t * P:S + (t + 1) * P], x1n[:, t, :], ident[:])
                    mm.then_inc(x1T_done, 1)

            def project_q(b):
                pe.wait_ge(xnT_taken, b + 1)
                nc.tensor.matmul(misc_ps[:, 0:S], w_qkvo[:, 0, :], xnT[:], start=True, stop=True).then_inc(q_done, 1)

            def project_k(b):
                pe.wait_ge(ctx_in, 16 * (b + 1))
                wait(pe, v_taken, b)
                wait(pe, heads_taken, b - 1)
                nc.tensor.matmul(misc_ps[:, S:2 * S], w_qkvo[:, 1, :], ctxT_in[:], start=True, stop=True).then_inc(k_done, 1)

            def project_v(b):
                for t in range(TT):
                    mm = nc.tensor.matmul(misc_ps[:, S + t * P:S + (t + 1) * P], ctxT_in[:, t * P:(t + 1) * P],
                                          w_qkvo[:, 2, :], start=True, stop=True)
                mm.then_inc(v_done, 1)

            def scores(b, u):
                n, kt, qt = UNITS * b + u, u // TT, u % TT
                if u == 0:
                    pe.wait_ge(k_stack_in, 32 * (b + 1))
                    pe.wait_ge(q_stack_in, 64 * (b + 1))
                wait(pe, exp_made, n - 1)
                for j in range(PAIRS):
                    mm = nc.tensor.matmul(
                        score_ps[:, u % 2, 2 * j * P:(2 * j + 2) * P], k_stack[:, j, kt * P:(kt + 1) * P],
                        q_stack[:, j, :, qt * P:(qt + 1) * P], start=(j % 2 == 0), stop=True,
                        skip_group_check=True)
                mm.then_inc(scores_done, 1)

            def subtract_max(b, u):
                pe.wait_ge(max_made, UNITS * b + u + 1)
                m4 = shift_m[:, u % 2, :].unsqueeze(1).to_broadcast([P, BANK // P, P])
                for half in range(2):
                    mm = nc.tensor.matmul(score_ps[:, u % 2, half * BANK:(half + 1) * BANK], neg_ident[:], m4,
                                          start=False, stop=True, skip_group_check=True)
                    if u == UNITS - 2 and half == 0:
                        mm.then_inc(stacks_free, 16)
                mm.then_inc(shifted, 1)

            def wait_for_b2_or_q(i, prepare, new):
                if new:
                    pe.wait_ge(b2_added, i)
                elif prepare:
                    pe.wait_ge(q_hi_made, i + 2)
                    pe.wait_ge(q_lo_made, i + 2)

            def attend_values(b):
                pe.wait_ge(attn0_made, b + 1)
                pe.wait_ge(attn_made, (UNITS - 1) * (b + 1))
                pe.wait_ge(v_taken, b + 1)
                for odd in range(2):
                    for kt in range(TT):
                        for g in range(PAIRS):
                            h = 2 * g + odd
                            mm = nc.tensor.matmul(misc_ps[32 * g:32 * g + 32, 0:S], v_pad[:, kt, h, :],
                                                  attn[:, kt, h, :], start=(odd == 0 and kt == 0),
                                                  stop=(odd == 1 and kt == TT - 1))
                mm.then_inc(av_done, 1)

            def project_out(b, attend):
                pe.wait_ge(heads_taken, b + 1)
                if attend:
                    pe.wait_ge(v_taken, b + 2)
                for t in range(TT):
                    mm = nc.tensor.matmul(misc_ps[:, t * P:(t + 1) * P], headsT[:, t * P:(t + 1) * P],
                                          w_qkvo[:, 3, :], start=True, stop=True)
                mm.then_inc(wo_done, 1)

            def route(b):
                if isinstance(b, int) and b == 0:
                    pe.wait_ge(wr_hi_made, 1)
                    pe.wait_ge(wr_lo_made, 1)
                for t in range(TT):
                    for n, (xt, w) in enumerate(((x1T_lo, wr_hi), (x1T_hi, wr_lo), (x1T_hi, wr_hi))):
                        mm = nc.tensor.matmul(misc_ps[:, S + t * E:S + (t + 1) * E], xt[:, t * P:(t + 1) * P], w[:],
                                              start=(n == 0), stop=(n == 2))
                mm.then_inc(router_done, 1)

            def project_q_and_route(b1, b2):
                if b2 is not None:
                    pe.wait_ge(x1T_hi_made, b2 + 1)
                    pe.wait_ge(x1T_lo_made, b2 + 1)
                if b1 is not None:
                    project_q(b1)
                if b2 is not None:
                    route(b2)

            def transpose_gates(b, prepare):
                pe.wait_ge(gates_made, b + 1)
                if prepare:
                    pe.wait_ge(q_hi_made, b + 3)
                    pe.wait_ge(q_lo_made, b + 3)
                for t in range(TT):
                    mm = nc.tensor.transpose(misc_ps[0:E, t * P:(t + 1) * P], gates[:, t, :], ident[:])
                mm.then_inc(gatesT_done, 1)

            def gated_b2(b):
                pe.wait_ge(gatesT_taken, b + 1)
                for t in range(TT):
                    mm = nc.tensor.matmul(misc_ps[:, t * P:(t + 1) * P], gatesT[:, t * P:(t + 1) * P], b2_sb[:],
                                          start=True, stop=True)
                mm.then_inc(b2_done, 1)

            def expert_up(b, e):
                n = E * b + e
                if e == 0:
                    pe.wait_ge(x1T_hi_made, b + 1)
                    pe.wait_ge(x1T_lo_made, b + 1)
                if e == 0 and isinstance(b, int) and b == 0:
                    pe.wait_ge(w1_hi_made, 2)
                    pe.wait_ge(w1_lo_made, 2)
                wait(pe, relu_made, n)
                for c in range(HC):
                    for k, (w, xt) in enumerate(((w1_lo, x1T_hi), (w1_hi, x1T_lo), (w1_hi, x1T_hi))):
                        mm = nc.tensor.matmul(h_ps[:, c * S:(c + 1) * S], w[:, e, c * P:(c + 1) * P], xt[:],
                                              start=(k == 0), stop=(k == 2))
                mm.then_inc(h_done, 1)

            def expert_down(b, e):
                n = E * b + e
                if e == 0 and isinstance(b, int) and b == 0:
                    pe.wait_ge(w2_in, 16)
                pe.wait_ge(relu_made, n + 1)
                wait(pe, gated, n - 1)
                for t in range(TT):
                    for c in range(HC):
                        mm = nc.tensor.matmul(y_ps[:, e % 2, t * D:(t + 1) * D], hT[:, e % 2, c, t * P:(t + 1) * P],
                                              w2_sb[:, e * HC + c, :], start=(c == 0), stop=(c == HC - 1))
                mm.then_inc(y_done, 1)

            def up(i, slot, new, old):
                if at := expert_up_at(slot, new, old):
                    expert_up(i - at[0], at[1])

            def down(i, slot, new, old):
                if at := expert_down_at(slot, new, old):
                    expert_down(i - at[0], at[1])

            def first_step():
                project_k(1)
                subtract_max(0, 0)
                subtract_max(0, 1)
                transpose_tokens(1, None)
                scores(0, 2)
                project_q_and_route(1, None)
                scores(0, 3)
                subtract_max(0, 2)
                subtract_max(0, 3)
                wait_for_b2_or_q(0, True, False)
                project_v(1)
                scores(1, 0)
                attend_values(0)
                scores(1, 1)

            def step(i, attend, prepare, new, old):
                if prepare and not new:
                    first_step()
                    return
                f = i - 1 if new else None
                coming = i + 1 if prepare else None
                up(i, 0, new, old)
                if prepare:
                    project_k(i + 1)
                if new:
                    project_out(f, attend)
                if attend:
                    subtract_max(i, 0)
                down(i, 0, new, old)
                up(i, 1, new, old)
                if attend:
                    scores(i, 2)
                    subtract_max(i, 1)
                down(i, 1, new, old)
                up(i, 2, new, old)
                if attend:
                    scores(i, 3)
                transpose_tokens(coming, f)
                down(i, 2, new, old)
                if attend:
                    subtract_max(i, 2)
                project_q_and_route(coming, f)
                up(i, 3, new, old)
                if attend:
                    subtract_max(i, 3)
                down(i, 3, new, old)
                up(i, 4, new, old)
                down(i, 4, new, old)
                up(i, 5, new, old)
                if new:
                    transpose_gates(f, prepare)
                down(i, 5, new, old)
                up(i, 6, new, old)
                if new:
                    gated_b2(f)
                down(i, 6, new, old)
                up(i, 7, new, old)
                if prepare:
                    scores(i + 1, 0)
                wait_for_b2_or_q(i, prepare, new)
                if prepare:
                    project_v(i + 1)
                down(i, 7, new, old)
                if attend:
                    attend_values(i)
                if prepare:
                    scores(i + 1, 1)

            pe.wait_ge(ident_made, 1)
            pe.wait_ge(wq_in, 16)
            project_k(0)
            transpose_tokens(0, None)
            project_q(0)
            pe.wait_ge(q_hi_made, 1)
            pe.wait_ge(q_lo_made, 1)
            project_v(0)
            scores(0, 0)
            scores(0, 1)
            pe.wait_ge(neg_ident_made, 1)
            pe.wait_ge(small_in, 64)
            pipeline(pe, step)

        @block.scalar
        def _(act):
            def take(dst, src, done, b, made):
                act.wait_ge(done, b + 1)
                nc.scalar.activation(dst, src, ACT.Copy).then_inc(made, 1)

            def take_xnT(b, new):
                if new:
                    act.wait_ge(x1T_done, b - 1)
                wait(act, q_done, b)
                take(xnT[:], misc_ps[:, 0:S], xnT_done, b, xnT_taken)

            def take_q_hi(b, new):
                if new:
                    act.wait_ge(router_done, b - 1)
                wait(act, q_spilled, 16 * b)
                take(q_parts[:, 0, :], misc_ps[:, 0:S], q_done, b, q_hi_made)

            def take_k_hi(b, new):
                if new:
                    act.wait_ge(x1_made, b - 1)
                wait(act, k_spilled, 16 * b)
                take(k_parts[:, 0, :], misc_ps[:, S:2 * S], k_done, b, k_hi_made)

            def take_v(b):
                wait(act, av_done, b)
                if isinstance(b, int) and b == 0:
                    act.wait_ge(v_zeroed, 1)
                dst = v_pad[:].rearrange("p k (j o) (a d) -> p (k j) (o a) d", o=2, d=DH)[:, :, 0:4:3, :]
                take(dst, misc_ps[:, S:2 * S].rearrange("p (n o d) -> p n o d", o=2, d=DH), v_done, b, v_taken)

            def exponentiate(b, u):
                n = UNITS * b + u
                act.wait_ge(shifted, n + 1)
                if u == 0:
                    wait(act, attn0_made, b)
                else:
                    wait(act, attn_made, (UNITS - 1) * (b - 1) + u)
                nc.scalar.activation(e_sb[:, u, :], score_ps[:, u % 2, :], ACT.Exp, scale=SCALE).then_inc(exp_made, 1)

            def invert_sum(b, u):
                n = UNITS * b + u
                act.wait_ge(sum_made, n + 1)
                nc.scalar.activation(log_sum[:, u, :], e_sum[:, u, :], ACT.Ln).then_inc(log_made, 1)
                act.wait_ge(log_made, n + 1)
                nc.scalar.activation(e_rcp[:, u, :], log_sum[:, u, :], ACT.Exp, scale=-1.0).then_inc(rcp_made, 1)

            def take_heads(b):
                wait(act, wo_done, b)
                take(headsT[:], misc_ps[:, 0:S], av_done, b, heads_taken)

            def take_x1T_hi(b):
                wait(act, h_done, E * b)
                take(x1T_hi[:], misc_ps[:, S:2 * S], x1T_done, b, x1T_hi_made)

            def router_exp(b):
                act.wait_ge(rel_made, b + 1)
                nc.scalar.activation(rel_exp[:], rel[:], ACT.Exp).then_inc(rel_exp_made, 1)

            def take_gatesT(b):
                wait(act, b2_done, b)
                take(gatesT[:], misc_ps[0:E, 0:S], gatesT_done, b, gatesT_taken)

            def relu(b, e):
                n = E * b + e
                act.wait_ge(h_done, n + 1)
                wait(act, y_done, n - 1)
                for c in range(HC):
                    op = nc.scalar.activation(hT[:, e % 2, c, :], h_ps[:, c * S:(c + 1) * S], ACT.Relu,
                                              bias=b1_sb[:, e * HC + c:e * HC + c + 1])
                op.then_inc(relu_made, 1)

            def relu_at(i, slot, new, old):
                if up := expert_up_at(slot, new, old):
                    relu(i - up[0], up[1])

            def first_step():
                take_k_hi(1, False)
                exponentiate(0, 0)
                exponentiate(0, 1)
                take_xnT(1, False)
                exponentiate(0, 2)
                take_q_hi(1, False)
                exponentiate(0, 3)
                invert_sum(0, 0)
                invert_sum(0, 1)
                split_w1()
                invert_sum(0, 2)
                invert_sum(0, 3)
                take_heads(0)
                take_v(1)

            def step(i, attend, prepare, new, old):
                if prepare and not new:
                    first_step()
                    return
                f = i - 1
                relu_at(i, 0, new, old)
                if attend:
                    exponentiate(i, 0)
                relu_at(i, 1, new, old)
                if prepare:
                    take_k_hi(i + 1, new)
                if attend:
                    exponentiate(i, 1)
                if prepare:
                    take_xnT(i + 1, new)
                if new:
                    take_x1T_hi(f)
                relu_at(i, 2, new, old)
                if attend:
                    exponentiate(i, 2)
                if prepare:
                    take_q_hi(i + 1, new)
                relu_at(i, 3, new, old)
                if attend:
                    exponentiate(i, 3)
                if new:
                    router_exp(f)
                relu_at(i, 4, new, old)
                if attend:
                    invert_sum(i, 0)
                    invert_sum(i, 1)
                relu_at(i, 5, new, old)
                if new:
                    take_gatesT(f)
                if attend:
                    invert_sum(i, 2)
                relu_at(i, 6, new, old)
                if attend:
                    invert_sum(i, 3)
                relu_at(i, 7, new, old)
                if prepare:
                    take_v(i + 1)
                if attend:
                    take_heads(i)

            def split_w1():
                act.wait_ge(w1_in, 16)
                for half in range(0, E, E // 2):
                    nc.scalar.activation(w1_hi[:, half:half + E // 2, :], w1_sb[:, half:half + E // 2, :],
                                         ACT.Copy).then_inc(w1_hi_made, 1)

            nc.scalar.preload_act_table_set("natural_log_exp_and_others")
            take_k_hi(0, False)
            take_xnT(0, False)
            take_q_hi(0, False)
            take_v(0)
            act.wait_ge(small_in, 64)
            pipeline(act, step)

        @block.vector
        def _(dve):
            def norm_stats(src, stats, step_sem):
                for t in range(TT):
                    op = nc.vector.bn_stats(stats[:, t, :], src[:, t, :])
                op.then_inc(step_sem, 1)

            def norm_vars(b1, b2):
                if b1 is not None:
                    dve.wait_ge(ln1_step, 2 * b1 + 1)
                if b2 is not None:
                    dve.wait_ge(x1_made, b2 + 1)
                    norm_stats(x1, ln2_stats, ln2_step)
                if b1 is not None:
                    for t in range(TT):
                        op = nc.vector.bn_aggr(ln1_mv[:, t, :], ln1_stats[:, t, :])
                    op.then_inc(ln1_step, 1)
                    dve.wait_ge(ln1_step, 2 * b1 + 2)
                    if b2 is not None:
                        dve.wait_ge(ln2_step, 2 * b2 + 1)
                    nc.vector.tensor_scalar(ln1_var[:], ln1_mv[:, :, 1], EPS, None, ALU.add).then_inc(ln1_var_made, 1)
                if b2 is not None:
                    if b1 is None:
                        dve.wait_ge(ln2_step, 2 * b2 + 1)
                    for t in range(TT):
                        op = nc.vector.bn_aggr(ln2_mv[:, t, :], ln2_stats[:, t, :])
                    op.then_inc(ln2_step, 1)
                    dve.wait_ge(ln2_step, 2 * b2 + 2)
                    nc.vector.tensor_scalar(ln2_var[:], ln2_mv[:, :, 1], EPS, None, ALU.add).then_inc(ln2_var_made, 1)

            def ln1_begin(b):
                dve.wait_ge(x_ln_in, 16 * (b + 1))
                norm_stats(x_ln, ln1_stats, ln1_step)

            def add_residual(b):
                dve.wait_ge(wo_done, b + 1)
                dve.wait_ge(x_res_in, 16 * (b + 1))
                wait(dve, gated, E * b - E + 1)
                nc.vector.tensor_tensor(x1[:].rearrange("p t d -> p (t d)"), misc_ps[:, 0:S],
                                        x_res[:].rearrange("p t d -> p (t d)"), ALU.add).then_inc(x1_made, 1)

            def ln2_end(b):
                dve.wait_ge(ln2_rstd_made, b + 1)
                wait(dve, x1T_done, b)
                for t in range(TT):
                    op = nc.vector.tensor_scalar(x1n[:, t, :], x1[:, t, :], ln2_mv[:, t, 0:1], ln2_rstd[:, t:t + 1],
                                                 ALU.subtract, ALU.mult)
                op.then_inc(x1n_made, 1)

            def low_part(dst, half, hi, hi_made, b, made):
                dve.wait_ge(hi_made, b + 1)
                nc.vector.tensor_tensor(dst, misc_ps[:, half * S:(half + 1) * S], hi.bitcast(F32), ALU.subtract).then_inc(made, 1)

            def q_lo(b):
                low_part(q_parts[:, 1, :], 0, q_parts[:, 0, :], q_hi_made, b, q_lo_made)

            def k_lo(b):
                low_part(k_parts[:, 1, :], 1, k_parts[:, 0, :], k_hi_made, b, k_lo_made)

            def x1T_low(b):
                wait(dve, h_done, E * b)
                low_part(x1T_lo[:], 1, x1T_hi[:], x1T_hi_made, b, x1T_lo_made)

            def head_max(b, u):
                dve.wait_ge(scores_done, UNITS * b + u + 1)
                nc.vector.tensor_reduce(shift_m[:, u % 2, :], score_ps[:, u % 2, :].rearrange("p (h q) -> p q h", h=H),
                                        AX.X, ALU.max).then_inc(max_made, 1)

            def normalize(b, u):
                kt, qt = u // TT, u % TT
                dve.wait_ge(rcp_made, UNITS * b + u + 1)
                if u == 1:
                    wait(dve, av_done, b)
                nc.vector.tensor_tensor(attn[:, kt, :, qt * P:(qt + 1) * P],
                                        e_sb[:, u, :].rearrange("p (h q) -> p h q", h=H),
                                        e_rcp[:, u, :].unsqueeze(1).to_broadcast([P, H, P]),
                                        ALU.mult).then_inc(attn_made, 1)

            def take_logits(b, prepare):
                dve.wait_ge(router_done, b + 1)
                if prepare:
                    dve.wait_ge(q_hi_made, b + 3)
                nc.vector.tensor_tensor(logits[:], misc_ps[:, S:S + TT * E].rearrange("p (t e) -> p t e", e=E),
                                        br_sb[:].unsqueeze(1).to_broadcast([P, TT, E]), ALU.add).then_inc(logits_made, 1)

            def choose_experts(b):
                at = ROUTER_STEPS * b
                for t in range(TT):
                    op = nc.vector.max(top8[:, t, :], logits[:, t, :])
                op.then_inc(router_step, 1)
                dve.wait_ge(router_step, at + 1)
                nc.vector.tensor_tensor(rel[:], logits[:], top8[:, :, 0:1].to_broadcast([P, TT, E]),
                                        ALU.subtract).then_inc(rel_made, 1)
                for t in range(TT):
                    op = nc.vector.max_index(top8_at[:, t, :], top8[:, t, :], logits[:, t, :])
                op.then_inc(router_step, 1)
                dve.wait_ge(router_step, at + 2)
                nc.vector.tensor_copy(top8_at_f[:], top8_at[:]).then_inc(router_step, 1)
                dve.wait_ge(router_step, at + 3)
                for n, place in enumerate((first, second)):
                    nc.vector.tensor_tensor(place[:], iota8[:].unsqueeze(1).to_broadcast([P, TT, E]),
                                            top8_at_f[:, :, n:n + 1].to_broadcast([P, TT, E]),
                                            ALU.is_equal).then_inc(router_step, 1)
                dve.wait_ge(router_step, at + 5)
                nc.vector.tensor_tensor(chosen[:], first[:], second[:], ALU.add).then_inc(router_step, 1)

            def make_gates(b):
                at = ROUTER_STEPS * b
                dve.wait_ge(rel_exp_made, b + 1)
                dve.wait_ge(router_step, at + 6)
                nc.vector.tensor_tensor(chosen_exp[:], rel_exp[:], chosen[:], ALU.mult).then_inc(router_step, 1)
                dve.wait_ge(router_step, at + 7)
                nc.vector.tensor_reduce(gate_sum[:], chosen_exp[:], AX.X, ALU.add).then_inc(router_step, 1)
                dve.wait_ge(router_step, at + 8)
                nc.vector.reciprocal(gate_rcp[:], gate_sum[:]).then_inc(router_step, 1)
                dve.wait_ge(router_step, at + 9)
                nc.vector.tensor_tensor(gates[:], chosen_exp[:], gate_rcp[:].unsqueeze(2).to_broadcast([P, TT, E]),
                                        ALU.mult).then_inc(gates_made, 1)

            def add_expert(b, e):
                n = E * b + e
                dve.wait_ge(y_done, n + 1)
                wait(dve, gated, n)
                if e == 0:
                    dve.wait_ge(gates_made, b + 1)
                if e == B2_AFTER + 1:
                    dve.wait_ge(b2_added, b + 1)
                if e == E - 1:
                    dve.wait_ge(stored, 16 * (b + 1))
                src = x1 if e == 0 else acc
                dst = y_out if e == E - 1 else acc
                for t in range(TT):
                    op = nc.vector.scalar_tensor_tensor(out=dst[:, t, :], in0=y_ps[:, e % 2, t * D:(t + 1) * D],
                                                        scalar=gates[:, t, e:e + 1], in1=src[:, t, :],
                                                        op0=ALU.mult, op1=ALU.add)
                op.then_inc(gated, 1)

            def add_b2(b):
                dve.wait_ge(b2_done, b + 1)
                dve.wait_ge(gated, E * b + B2_AFTER + 1)
                nc.vector.tensor_tensor(acc[:].rearrange("p t d -> p (t d)"), misc_ps[:, 0:S],
                                        acc[:].rearrange("p t d -> p (t d)"), ALU.add).then_inc(b2_added, 1)

            def step(i, attend, prepare, new, old):
                if prepare and not new:
                    first_step()
                    return
                f, g = i - 1, i - 2
                if attend:
                    head_max(i, 1)
                if prepare:
                    ln1_begin(i + 1)
                if new:
                    add_residual(f)
                norm_vars(i + 1 if prepare else None, f if new else None)
                if old:
                    add_expert(g, 4)
                if prepare:
                    k_lo(i + 1)
                if new:
                    ln2_end(f)
                if attend:
                    head_max(i, 2)
                if old:
                    add_expert(g, 5)
                if new:
                    x1T_low(f)
                if attend:
                    head_max(i, 3)
                if old:
                    add_expert(g, 6)
                if new:
                    take_logits(f, prepare)
                    dve.wait_ge(logits_made, f + 1)
                if prepare:
                    q_lo(i + 1)
                if new:
                    choose_experts(f)
                if old:
                    add_expert(g, 7)
                if new:
                    make_gates(f)
                    add_expert(f, 0)
                if attend:
                    normalize(i, 1)
                if new:
                    add_expert(f, 1)
                if attend:
                    normalize(i, 2)
                if new:
                    add_b2(f)
                if attend:
                    normalize(i, 3)
                if new:
                    add_expert(f, 2)
                    add_expert(f, 3)
                if prepare:
                    head_max(i + 1, 0)

            def first_step():
                head_max(0, 1)
                k_lo(1)
                head_max(0, 2)
                head_sum(0, 1)
                q_lo(1)
                head_max(0, 3)
                normalize(0, 1)
                head_sum(0, 2)
                head_sum(0, 3)
                normalize(0, 2)
                normalize(0, 3)
                head_max(1, 0)

            def head_sum(b, u):
                n = UNITS * b + u
                dve.wait_ge(exp_made, n + 1)
                dve.wait_ge(sum_made, n)
                nc.vector.tensor_reduce(e_sum[:, u, :], e_sb[:, u, :].rearrange("p (h q) -> p q h", h=H),
                                        AX.X, ALU.add).then_inc(sum_made, 1)

            nc.vector.memset(q_stack[:].bitcast(F32), 0.0).then_inc(stacks_free, 16)
            ln1_begin(0)
            norm_vars(0, None)
            dve.wait_ge(ln1_rstd_made, 1)
            for t in range(TT):
                op = nc.vector.tensor_scalar(xn[:, t, :], x_ln[:, t, :], ln1_mv[:, t, 0:1], ln1_rstd[:, t:t + 1],
                                             ALU.subtract, ALU.mult)
            op.then_inc(xn_made, 1)
            dve.wait_ge(ident_made, 1)
            nc.vector.tensor_scalar(neg_ident[:], ident[:], -1.0, None, ALU.mult).then_inc(neg_ident_made, 1)
            k_lo(0)
            nc.vector.memset(v_pad[:], 0.0).then_inc(v_zeroed, 1)
            q_lo(0)
            nc.vector.memset(y_out[:], 0.0).then_inc(stored, 16)
            dve.wait_ge(small_in, 64)
            nc.vector.tensor_copy(wr_hi[:], wr_sb[:]).then_inc(wr_hi_made, 1)
            dve.wait_ge(wr_hi_made, 1)
            nc.vector.tensor_tensor(wr_lo[:], wr_sb[:], wr_hi[:].bitcast(F32), ALU.subtract).then_inc(wr_lo_made, 1)
            ln1_begin(1)
            norm_vars(1, None)
            dve.wait_ge(pool_made, 1)
            head_max(0, 0)
            pipeline(dve, step)

        @block.gpsimd
        def _(pool):
            def rstd(b, var, var_made, dst, made):
                pool.wait_ge(var_made, b + 1)
                nc.gpsimd.tensor_tensor(dst[:], var[:], neg_half[:], ALU.pow).then_inc(made, 1)

            def centre(b):
                pool.wait_ge(ln1_var_made, b + 1)
                nc.gpsimd.tensor_tensor(x_centred[:], x_ln[:], ln1_mv[:, :, 0:1].to_broadcast([P, TT, D]),
                                        ALU.subtract).then_inc(centred, 1)

            def ln1_rstd_of(b):
                rstd(b, ln1_var, ln1_var_made, ln1_rstd, ln1_rstd_made)

            def ln1_end(b):
                pool.wait_ge(centred, b)
                pool.wait_ge(ln1_rstd_made, b + 1)
                wait(pool, xnT_done, b)
                nc.gpsimd.tensor_tensor(xn[:], x_centred[:], ln1_rstd[:].unsqueeze(2).to_broadcast([P, TT, D]),
                                        ALU.mult).then_inc(xn_made, 1)

            def head_sum(b, u):
                n = UNITS * b + u
                at = 0 if isinstance(n, int) and n == 0 else 2 * (n - SUMS_BY_DVE)
                pool.wait_ge(exp_made, n + 1)
                e = e_sb[:, u, :]
                nc.gpsimd.tensor_tensor(half_sum[:], e[:, 0:HQ // 2], e[:, HQ // 2:HQ], ALU.add).then_inc(sum_step, 1)
                pool.wait_ge(sum_step, at + 1)
                nc.gpsimd.tensor_tensor(quarter_sum[:], half_sum[:, 0:HQ // 4], half_sum[:, HQ // 4:HQ // 2],
                                        ALU.add).then_inc(sum_step, 1)
                pool.wait_ge(sum_step, at + 2)
                if isinstance(n, int) and n == UNITS:
                    pool.wait_ge(sum_made, n)
                nc.gpsimd.tensor_tensor(e_sum[:, u, :], quarter_sum[:, 0:P], quarter_sum[:, P:2 * P],
                                        ALU.add).then_inc(sum_made, 1)

            def normalize(b, u):
                kt, qt = u // TT, u % TT
                pool.wait_ge(rcp_made, UNITS * b + u + 1)
                wait(pool, av_done, b)
                nc.gpsimd.tensor_tensor(attn[:, kt, :, qt * P:(qt + 1) * P],
                                        e_sb[:, u, :].rearrange("p (h q) -> p h q", h=H),
                                        e_rcp[:, u, :].unsqueeze(1).to_broadcast([P, H, P]),
                                        ALU.mult).then_inc(attn0_made, 1)

            def step(i, attend, prepare, new, old):
                if prepare and not new:
                    first_step()
                    return
                f = i - 1
                if prepare:
                    centre(i + 1)
                if new:
                    rstd(f, ln2_var, ln2_var_made, ln2_rstd, ln2_rstd_made)
                if prepare:
                    ln1_rstd_of(i + 1)
                    ln1_end(i + 1)
                if attend:
                    head_sum(i, 0)
                    head_sum(i, 1)
                    head_sum(i, 2)
                    head_sum(i, 3)
                    normalize(i, 0)

            def first_step():
                head_sum(0, 0)
                normalize(0, 0)
                for half in range(2):
                    pool.wait_ge(w1_hi_made, half + 1)
                    part = slice(half * E // 2, (half + 1) * E // 2)
                    nc.gpsimd.tensor_tensor(w1_lo[:, part, :], w1_sb[:, part, :], w1_hi[:, part, :].bitcast(F32),
                                            ALU.subtract).then_inc(w1_lo_made, 1)

            nc.gpsimd.memset(neg_half[:], -0.5).then_inc(zeroed, 1)
            nc.gpsimd.memset(ident[:], 0.0).then_inc(zeroed, 1)
            pool.wait_ge(zeroed, 2)
            nc.gpsimd.affine_select(out=ident[:], in_=ident[:], compare_op=ALU.not_equal, fill=1.0, base=0,
                                    pattern=[[-1, P]], channel_multiplier=1).then_inc(ident_made, 1)
            ln1_rstd_of(0)
            for e in range(E):
                op = nc.gpsimd.memset(iota8[:, e:e + 1], float(e))
            op.then_inc(pool_made, 1)
            centre(1)
            ln1_rstd_of(1)
            ln1_end(1)
            pipeline(pool, step)


def kernel(x, ctx_1024, L0_xattn_W_Q, L0_xattn_W_K, L0_xattn_W_V, L0_xattn_W_O, L0_ffn_Wr, L0_ffn_br,
           L0_ffn_W1, L0_ffn_b1, L0_ffn_W2, L0_ffn_b2):
    import numpy as np
    import concourse.bacc as bacc
    from concourse.bass_utils import run_bass_kernel_spmd

    E, HID = L0_ffn_b1.shape
    w_attn = np.stack([np.asarray(w).T for w in (L0_xattn_W_Q, L0_xattn_W_K, L0_xattn_W_V, L0_xattn_W_O)], axis=1)
    given = {
        "x": x,
        "ctx_t": np.asarray(ctx_1024).transpose(0, 2, 1),
        "w_attn": w_attn,
        "wr": L0_ffn_Wr,
        "br": L0_ffn_br,
        "w1": L0_ffn_W1,
        "b1_t": np.asarray(L0_ffn_b1).reshape(E * HID // P, P).T,
        "w2": L0_ffn_W2,
        "b2": L0_ffn_b2,
    }
    nc = bacc.Bacc("TRN2", target_bir_lowering=False, num_devices=1)
    arrays, args = {}, []
    for name, a in given.items():
        a = np.ascontiguousarray(a)
        arrays[f"in_{name}"] = a
        args.append(nc.dram_tensor(f"in_{name}", a.shape, mybir.dt.from_np(a.dtype), kind="ExternalInput").ap())
    shape = tuple(np.asarray(x).shape)
    args.append(nc.dram_tensor("out_y", shape, F32, kind="ExternalOutput").ap())
    build(nc, *args)
    r = run_bass_kernel_spmd(nc, [arrays], core_ids=[0])
    return r.results[0]["out_y"]
```
